# Optimizing a Trainium2 kernel written in Bass

```python
import numpy as np
import jax
import jax.numpy as jnp

def _softmax(x, axis=-1):
    return jax.nn.softmax(x, axis=axis)

def _gelu(x):
    return jax.nn.gelu(x, approximate=True)

def _silu(x):
    return jax.nn.silu(x)

def _sigmoid(x):
    return jax.nn.sigmoid(x)

def _layernorm(x, axis=-1, eps=1e-05):
    m = jnp.mean(x, axis=axis, keepdims=True)
    v = jnp.var(x, axis=axis, keepdims=True)
    return (x - m) / jnp.sqrt(v + eps)

def _scatter_add(tgt, idx, src, axis=0):
    return tgt.at[idx].add(src)

def _segment_sum(src, seg, n):
    return jax.ops.segment_sum(src, seg, n)
kernel_name = 'mk_seq_preln_d1_jaxref_r8_61f6dc'

def setup_inputs(seed: int=0):
    np.random.seed(seed)
    _w = jnp.asarray

    def _L0_attn_setup():
        import jax, jax.numpy as jnp
        import numpy as np
        N_HEADS = 16
        HEAD_DIM = 64
        ROPE_THETA = 10000.0
        EPS = 1e-06

        def _rmsnorm(x, w):
            rms = jnp.sqrt(jnp.mean(jnp.square(x), axis=-1, keepdims=True) + EPS)
            return x / rms * w

        def _rope(x, cos, sin):
            x1, x2 = jnp.split(x, 2, axis=-1)
            return jnp.concatenate([x1 * cos - x2 * sin, x1 * sin + x2 * cos], axis=-1)
        key = jax.random.key(seed)
        ks = jax.random.split(key, 3)
        B, T, C = (2, 256, 128)
        x = jax.random.normal(ks[0], (B, T, C), dtype=jnp.float32)
        wqkv = jax.random.normal(ks[1], (3 * N_HEADS * HEAD_DIM, C), dtype=jnp.float32) * C ** (-0.5)
        wo = jax.random.normal(ks[2], (C, N_HEADS * HEAD_DIM), dtype=jnp.float32) * (N_HEADS * HEAD_DIM) ** (-0.5)
        q_norm_w = jnp.ones((HEAD_DIM,), dtype=jnp.float32)
        k_norm_w = jnp.ones((HEAD_DIM,), dtype=jnp.float32)
        return {'x': x, 'wqkv': wqkv, 'wo': wo, 'q_norm_w': q_norm_w, 'k_norm_w': k_norm_w}
    _L0_attn_in = _L0_attn_setup()

    def _L0_ffn_setup():
        import math
        import jax, jax.numpy as jnp
        import numpy as np
        NUM_EXPERTS = 16
        TOP_K = 2
        CAPACITY_FACTOR = 1.25
        key = jax.random.key(seed)
        k1, k2, k3, k4 = jax.random.split(key, 4)
        d, dff, E = (128, 512, NUM_EXPERTS)
        x = jax.random.normal(k1, (4, 256, d), dtype=jnp.float32)
        router_w = jax.random.normal(k2, (E, d), dtype=jnp.float32) * d ** (-0.5)
        router_b = jnp.zeros((E,), dtype=jnp.float32)
        w1 = jax.random.normal(k3, (E, d, dff), dtype=jnp.float32) * 0.02
        b1 = jnp.zeros((E, dff), dtype=jnp.float32)
        w2 = jax.random.normal(k4, (E, dff, d), dtype=jnp.float32) * 0.02
        b2 = jnp.zeros((E, d), dtype=jnp.float32)
        return {'x': x, 'router_w': router_w, 'router_b': router_b, 'w1': w1, 'b1': b1, 'w2': w2, 'b2': b2}
    _L0_ffn_in = _L0_ffn_setup()
    _d = {'L0_attn_x': _L0_attn_in['x'], 'L0_attn_wqkv': _L0_attn_in['wqkv'], 'L0_attn_wo': _L0_attn_in['wo'], 'L0_attn_q_norm_w': _L0_attn_in['q_norm_w'], 'L0_attn_k_norm_w': _L0_attn_in['k_norm_w'], 'L0_ffn_router_w': _L0_ffn_in['router_w'], 'L0_ffn_router_b': _L0_ffn_in['router_b'], 'L0_ffn_w1': _L0_ffn_in['w1'], 'L0_ffn_b1': _L0_ffn_in['b1'], 'L0_ffn_w2': _L0_ffn_in['w2'], 'L0_ffn_b2': _L0_ffn_in['b2']}
    _x0 = _d['L0_attn_x']
    _d['L0_attn_x'] = jax.random.normal(jax.random.fold_in(jax.random.key(seed), 1), (8, 512, 128), dtype=_x0.dtype)
    del _x0
    return _d

def reference(L0_attn_x, L0_attn_wqkv, L0_attn_wo, L0_attn_q_norm_w, L0_attn_k_norm_w, L0_ffn_router_w, L0_ffn_router_b, L0_ffn_w1, L0_ffn_b1, L0_ffn_w2, L0_ffn_b2):

    def _L0_attn_ref(x, wqkv, wo, q_norm_w, k_norm_w):
        import jax, jax.numpy as jnp
        import numpy as np
        N_HEADS = 16
        HEAD_DIM = 64
        ROPE_THETA = 10000.0
        EPS = 1e-06

        def _rmsnorm(x, w):
            rms = jnp.sqrt(jnp.mean(jnp.square(x), axis=-1, keepdims=True) + EPS)
            return x / rms * w

        def _rope(x, cos, sin):
            x1, x2 = jnp.split(x, 2, axis=-1)
            return jnp.concatenate([x1 * cos - x2 * sin, x1 * sin + x2 * cos], axis=-1)
        B, T, C = x.shape
        H, D = (N_HEADS, HEAD_DIM)
        qkv = jnp.einsum('btc,oc->bto', x, wqkv)
        q, k, v = jnp.split(qkv, 3, axis=-1)

        def to_heads(t):
            return t.reshape(B, T, H, D).transpose(0, 2, 1, 3)
        q, k, v = (to_heads(q), to_heads(k), to_heads(v))
        q = _rmsnorm(q, q_norm_w)
        k = _rmsnorm(k, k_norm_w)
        inv_freq = 1.0 / ROPE_THETA ** (jnp.arange(0, D, 2, dtype=jnp.float32) / D)
        freqs = jnp.arange(T, dtype=jnp.float32)[:, None] * inv_freq
        cos, sin = (jnp.cos(freqs), jnp.sin(freqs))
        q = _rope(q, cos, sin)
        k = _rope(k, cos, sin)
        scale = D ** (-0.5)
        attn = jnp.einsum('bhtd,bhsd->bhts', q, k) * scale
        causal = jnp.tril(jnp.ones((T, T), dtype=bool))
        attn = jnp.where(causal, attn, -jnp.inf)
        attn = jax.nn.softmax(attn.astype(jnp.float32), axis=-1).astype(q.dtype)
        out = jnp.einsum('bhts,bhsd->bhtd', attn, v)
        out = out.transpose(0, 2, 1, 3).reshape(B, T, H * D)
        return jnp.einsum('bte,ce->btc', out, wo)

    def _L0_ffn_ref(x, router_w, router_b, w1, b1, w2, b2):
        import math
        import jax, jax.numpy as jnp
        import numpy as np
        NUM_EXPERTS = 16
        TOP_K = 2
        CAPACITY_FACTOR = 1.25
        E, k = (NUM_EXPERTS, TOP_K)
        B, S, d = x.shape
        tokens = B * S
        capacity = max(1, int(math.ceil(CAPACITY_FACTOR * tokens * k / E)))
        x2d = x.reshape(tokens, d)
        logits = x2d @ router_w.T + router_b
        vals, idx = jax.lax.top_k(logits, k)
        gates = jax.nn.softmax(vals, axis=-1)
        flat_e = idx.reshape(-1)
        oh = (flat_e[:, None] == jnp.arange(E)[None, :]).astype(jnp.int32)
        pos = jnp.take_along_axis(jnp.cumsum(oh, axis=0) - 1, flat_e[:, None], axis=1)[:, 0]
        kept = pos < capacity
        kept2 = kept.reshape(tokens, k)
        denom = jnp.sum(gates * kept2, axis=-1, keepdims=True)
        gates = jnp.where(kept2, gates / (denom + 1e-09), 0.0)
        slot = flat_e * capacity + pos
        slot_safe = jnp.where(kept, slot, E * capacity)
        x_rep = jnp.repeat(x2d, k, axis=0)
        buf = jnp.zeros((E * capacity + 1, d), x.dtype).at[slot_safe].set(x_rep)
        packed = buf[:E * capacity].reshape(E, capacity, d)
        h = jax.nn.gelu(jnp.einsum('ecd,edf->ecf', packed, w1) + b1[:, None, :], approximate=False)
        expert_out = jnp.einsum('ecf,efd->ecd', h, w2) + b2[:, None, :]
        eflat = expert_out.reshape(E * capacity, d)
        gathered = eflat[jnp.clip(slot, 0, E * capacity - 1)]
        w = (gates.reshape(-1) * kept.astype(x.dtype))[:, None]
        out = (gathered * w).reshape(tokens, k, d).sum(axis=1)
        return out.reshape(B, S, d)
    x = L0_attn_x
    x = x + _L0_attn_ref(_layernorm(x, axis=-1), L0_attn_wqkv, L0_attn_wo, L0_attn_q_norm_w, L0_attn_k_norm_w)
    x = x + _L0_ffn_ref(_layernorm(x, axis=-1), L0_ffn_router_w, L0_ffn_router_b, L0_ffn_w1, L0_ffn_b1, L0_ffn_w2, L0_ffn_b2)
    return x

_drawn_inputs = setup_inputs


def setup_inputs(seed=0):
    import zlib

    import numpy as np

    out = dict(_drawn_inputs(seed))
    spreads = {'L0_attn_q_norm_w': (1.0, 0.2),
     'L0_attn_k_norm_w': (1.0, 0.2),
     'L0_ffn_router_b': (0.0, 0.294),
     'L0_ffn_b1': (0.0, 0.455),
     'L0_ffn_b2': (0.0, 0.1)}
    factors = {}
    for name, (base, spread) in spreads.items():
        noise = np.random.default_rng([zlib.crc32(name.encode()), seed]).standard_normal(out[name].shape)
        drawn = base * np.exp(spread * noise) if base else spread * noise
        out[name] = jnp.asarray(drawn.astype(out[name].dtype))
    for name, factor in factors.items():
        out[name] = (out[name] * factor).astype(out[name].dtype)
    return out
```

```python
import concourse.bass as bass
from concourse import mybir
from contextlib import ExitStack

F32 = mybir.dt.float32
BF16 = mybir.dt.bfloat16
U32 = mybir.dt.uint32
ALU = mybir.AluOpType
ACT = mybir.ActivationFunctionType
AX = mybir.AxisListType

P = 128
B, T, C = 8, 512, 128
H, D = 16, 64
TPB = T // P
NT = B * TPB
NP = H // 2
UNITS = B * NP
QKV = 3 * P
E, F, TOPK = 16, 512, 2
FC = F // P
CAP = -(-5 * B * T * TOPK // (4 * E))
SJ = CAP // P
HALF = CAP // 2
SLOTS = E * CAP
RMS_EPS, LN_EPS = 1e-6, 1e-5
MASKED = -1e30
LAG = 2
PROB_OFF = [P * q * (q + 1) // 2 for q in range(TPB)]
PROB_COLS = P * TPB * (TPB + 1) // 2

STEP, TAIL = "step", "tail"


def attention_schedule(eng):
    for s in (-2, -1, 0):
        yield STEP, s, 0
    with eng.Fori(0, B - 1) as b:
        with eng.Fori(0, NP // 2) as it:
            for k in (1, 2):
                yield STEP, Where(b * 8 + it * 2 + k, k % 2, it * 2 + (k - 1)), b
        yield TAIL, b, b
    with eng.Fori(0, 2) as it:
        for k in (1, 2):
            yield STEP, Where(it * 2 + (8 * (B - 1) + k), k % 2, it * 2 + (k - 1)), B - 1
    for s in range(UNITS - 3, UNITS + 1):
        yield STEP, s, B - 1
    yield TAIL, B - 1, B - 1


class Where:

    def __init__(self, number, parity, pair):
        self.number, self.parity, self.pair = number, parity, pair


def number_of(s):
    return s.number if isinstance(s, Where) else s


def parity_of(s):
    return s.parity if isinstance(s, Where) else s % 2


def pair_before(s):
    return s.pair if isinstance(s, Where) else (s - 1) % NP


def has_unit(s, offset):
    return isinstance(s, Where) or 0 <= s + offset < UNITS


def has_tile(s, q, lag):
    return isinstance(s, Where) or 0 <= 4 * s + q - lag < 4 * UNITS


def settle(eng, s_mark):
    eng.sem_inc(s_mark, 1)


def wait(eng, sem, value):
    if isinstance(value, int) and value <= 0:
        return
    eng.wait_ge(sem, value)


def build(nc, x_in, wqkv_in, wo_in, qw_in, kw_in, rw_in, rb_in, w1_in, b1_in, w2_in, b2_in, cos_in, sin_in, out):
    packed = nc.dram_tensor("packed", (SLOTS, C), F32, kind="Internal").ap()
    expert_out = nc.dram_tensor("expert_out", (SLOTS, C), F32, kind="Internal").ap()
    zero_rows = P * PROB_COLS * 2 // C
    x_tiles = x_in.rearrange("b (t p) c -> p b t c", p=P)
    out_tiles = out.rearrange("b (t p) c -> p b t c", p=P)

    with ExitStack() as ctx:
        def sb(name, shape, dt=F32):
            return ctx.enter_context(nc.sbuf_tensor(name, shape, dt))

        def psum(name, shape, dt=F32):
            return inner.enter_context(nc.psum_tensor(name, shape, dt))

        def sem(name):
            return ctx.enter_context(nc.semaphore(name))

        inner = ctx.enter_context(ExitStack())

        def sba(name, shape, dt=F32):
            return inner.enter_context(nc.sbuf_tensor(name, shape, dt))

        x = sb("x", [P, NT, C])
        xnT_all = sb("xnT_all", [P, NT, P])
        xn2 = xnT_all
        ident = sb("ident", [P, P])
        identb = sb("identb", [P, P], BF16)
        before = sb("before", [P, P], BF16)
        onesb = sb("onesb", [P, P], BF16)
        half = sb("half", [P, 1])
        stats = sb("stats", [P, 2, TPB, 6])
        mv = sb("mv", [P, 2, TPB, 2])
        lnv = sb("lnv", [P, 2, TPB])
        lnr = sb("lnr", [P, 2, TPB])
        lnx = sb("lnx", [P, 2, TPB, C])
        wqkv = sba("wqkv", [P, NP, QKV])
        wo = sba("wo", [P, NP, C])
        causal = sba("causal", [P, P], BF16)
        normw = sba("normw", [P, 2, D])
        cosw = sba("cosw", [P, TPB, 2, D])
        sinw = sba("sinw", [P, TPB, 2, D])
        cost = sba("cost", [P, TPB, D])
        sint = sba("sint", [P, TPB, D])
        wbuf = sba("wbuf", [P, 2, QKV])
        xbuf = sba("xbuf", [P, 2, T])
        raw = sba("raw", [P, 2, TPB, QKV])
        vbuf = sba("vbuf", [P, 2, TPB, P])
        sq = sba("sq", [P, TPB, 2 * P])
        ss = sba("ss", [P, TPB * 4])
        ssv = sba("ssv", [P, TPB * 4])
        rstd = sba("rstd", [P, TPB * 4])
        sc = sba("sc", [P, TPB, 2 * P])
        rot = sba("rot", [P, TPB, 2 * P])
        swp = sba("swp", [P, TPB, 2 * P])
        qkT = sba("qkT", [P, 2, 2, T])
        negm = sba("negm", [P, TPB, 2])
        psums = sba("psums", [P, TPB, 2])
        rinv = sba("rinv", [P, TPB, 2])
        prob = sba("prob", [P, 2, PROB_COLS])
        probT = sba("probT", [P, 2, TPB, T])
        outT = sba("outT", [P, NP, T])
        yT = sba("yT", [P, T])

        bank_s = psum("bank_s", [P, 2, 2, 512])
        bank_t = psum("bank_t", [P, 2, 512])
        bank_o = psum("bank_o", [P, 512])
        bank_m = psum("bank_m", [P, 512])

        s_load = sem("s_load")
        s_x = sem("s_x")
        s_const = sem("s_const")
        s_mark = sem("s_mark")
        s_tab = sem("s_tab")
        s_bn = sem("s_bn")
        s_mv = sem("s_mv")
        s_lnv = sem("s_lnv")
        s_lnr = sem("s_lnr")
        s_lnx = sem("s_lnx")
        s_lnT = sem("s_lnT")
        s_xnT = sem("s_xnT")
        s_w = [sem("s_w0"), sem("s_w1")]
        s_proj = sem("s_proj")
        s_raw = sem("s_raw")
        s_v = [sem("s_v0"), sem("s_v1")]
        s_sq = sem("s_sq")
        s_ss = sem("s_ss")
        s_ssv = sem("s_ssv")
        s_rstd = sem("s_rstd")
        s_sc = sem("s_sc")
        s_cos = sem("s_cos")
        s_sin = sem("s_sin")
        s_rope = sem("s_rope")
        s_qkTp = sem("s_qkTp")
        s_qkT = sem("s_qkT")
        s_scores = sem("s_scores")
        s_negm = sem("s_negm")
        s_exp = sem("s_exp")
        s_rinv = sem("s_rinv")
        s_norm = sem("s_norm")
        s_pt = sem("s_pt")
        s_probT = sem("s_probT")
        s_pv = sem("s_pv")
        s_outT = sem("s_outT")
        s_y = sem("s_y")
        s_yT = sem("s_yT")
        s_yt = sem("s_yt")
        s_x2 = sem("s_x2")
        s_zero = sem("s_zero")
        s_fill = sem("s_fill")

        def qk_heads(t):
            return t[:, :, :].rearrange("p t (a d) -> p t a d", d=D)

        def by_head(t):
            return t[:, :, :].rearrange("p t (a h d) -> p (t a) h d", a=2, h=2)

        def table(t):
            return t[:, :, :, :].rearrange("p t a d -> p (t a) d")

        def prob_tile(h, q):
            return prob[:, h, PROB_OFF[q]:PROB_OFF[q] + (q + 1) * P]

        with nc.Block() as block:

            @block.sync
            def _(sp):
                sp.dma_start(x[:, 0:TPB, :], x_tiles[:, 0, :, :]).then_inc(s_x, 16)
                for dst, src in ((cost[:, :, :], cos_in), (sint[:, :, :], sin_in),
                                 (normw[:, 0, :], qw_in.rearrange("(a d) -> a d", a=1).to_broadcast([P, D])),
                                 (normw[:, 1, :], kw_in.rearrange("(a d) -> a d", a=1).to_broadcast([P, D])),
                                 (wqkv[:, :, :], wqkv_in), (wo[:, :, :], wo_in)):
                    sp.dma_start(dst, src).then_inc(s_load, 16)
                with sp.Fori(1, B) as b:
                    sp.wait_ge(s_x, b * 16)
                    settle(sp, s_mark)
                    sp.dma_start(x[:, bass.ds(b * TPB, TPB), :],
                                 x_tiles[:, bass.ds(b, 1), :, :].rearrange("p b t c -> p (b t) c")).then_inc(s_x, 16)
                sp.wait_ge(s_zero, 1)
                for r in range(SLOTS // zero_rows):
                    sp.dma_start(packed[r * zero_rows:(r + 1) * zero_rows, :].rearrange("(p r) c -> p (r c)", p=P),
                                 prob[:, :, :].rearrange("p h n -> p (h n)")).then_inc(s_fill, 16)
                sp.wait_ge(s_fill, 16 * (SLOTS // zero_rows))
                sp.wait_ge(s_load, 16 * 6)

                def operands(b, p):
                    sp.wait_ge(s_xnT, b + 1)
                    sp.dma_start(wbuf[:, p % 2, :], wqkv[:, p, :]).then_inc(s_w[p % 2], 16)
                    xn = xnT_all[:, bass.ds(b * TPB, TPB), :] if not isinstance(b, int) else \
                        xnT_all[:, b * TPB:(b + 1) * TPB, :]
                    sp.dma_start(xbuf[:, p % 2, :], xn.rearrange("p t k -> p (t k)")).then_inc(s_w[p % 2], 16)

                def values(u, p):
                    wait(sp, s_raw, u * 4 + 4)
                    wait(sp, s_pv, u - 1)
                    sp.dma_start(vbuf[:, p % 2, :, :], raw[:, p % 2, :, 2 * P:QKV]).then_inc(s_v[p % 2], 16)

                operands(0, 0)
                operands(0, 1)
                values(0, 0)
                sp.wait_ge(s_proj, 4)
                operands(0, 2)
                with sp.Fori(0, B - 1) as b:
                    for p in range(1, NP + 1):
                        values(b * NP + p, p)
                        sp.wait_ge(s_proj, b * (4 * NP) + (4 * p + 4))
                        settle(sp, s_mark)
                        operands(b if p + 2 < NP else b + 1, (p + 2) % NP)
                for p in range(1, NP):
                    values((B - 1) * NP + p, p)
                    if p + 2 < NP:
                        sp.wait_ge(s_proj, 4 * ((B - 1) * NP + p) + 4)
                        operands(B - 1, p + 2)

            @block.gpsimd
            def _(pool):
                g = nc.gpsimd
                g.memset(prob[:, :, :], 0.0).then_inc(s_zero, 1)
                g.memset(half[:, :], -0.5)
                g.memset(ident[:, :], 0.0)
                g.memset(identb[:, :], 0.0)
                g.memset(causal[:, :], 0.0)
                g.memset(before[:, :], 1.0)
                g.memset(onesb[:, :], 1.0).then_inc(s_const, 1)
                pool.wait_ge(s_const, 1)
                for m in (ident, identb):
                    g.affine_select(out=m[:, :], in_=m[:, :], compare_op=ALU.not_equal, fill=1.0, base=0,
                                    pattern=[[-1, P]], channel_multiplier=1)
                g.affine_select(out=causal[:, :], in_=causal[:, :], compare_op=ALU.is_ge, fill=MASKED, base=0,
                                pattern=[[-1, P]], channel_multiplier=1)
                g.affine_select(out=before[:, :], in_=before[:, :], compare_op=ALU.is_gt, fill=0.0, base=0,
                                pattern=[[1, P]], channel_multiplier=-1).then_inc(s_const, 1)

                with pool.Fori(0, B // 2) as k:
                    for par in range(2):
                        ln_pool(nc, pool, k * 2 + par, par, mv, lnv, lnr, half, s_mark, s_mv, s_lnv, s_lnr)

                for kind, s, b in attention_schedule(pool):
                    if kind == TAIL:
                        continue
                    n = number_of(s)
                    for q in range(4):
                        if q == 0 and has_unit(s, 1):
                            wait(pool, s_ss, n + 2)
                            settle(pool, s_mark)
                            g.tensor_scalar(ssv[:, :], ss[:, :], 1.0 / D, RMS_EPS, ALU.mult, ALU.add).then_inc(s_ssv, 1)
                            wait(pool, s_ssv, n + 2)
                            g.tensor_tensor(out=rstd[:, :], in0=ssv[:, :], in1=half[:, 0:1].to_broadcast([P, 16]),
                                            op=ALU.pow).then_inc(s_rstd, 1)
                        if q == 2 and has_unit(s, 1):
                            wait(pool, s_sc, n + 2)
                            src, dst, tab = by_head(sc), by_head(swp), table(sinw)
                            for lo, hi in ((0, D // 2), (D // 2, 0)):
                                last = g.tensor_tensor(
                                    out=dst[:, :, :, lo:lo + D // 2], in0=src[:, :, :, hi:hi + D // 2],
                                    in1=tab[:, :, None, lo:lo + D // 2].to_broadcast([P, 8, 2, D // 2]), op=ALU.mult)
                            last.then_inc(s_sin, 1)

            @block.vector
            def _(dve):
                v = nc.vector
                dve.sem_inc(s_x2, 1)
                dve.wait_ge(s_load, 16 * 6)
                for a in range(2):
                    scale = D ** -0.5 if a == 0 else 1.0
                    v.scalar_tensor_tensor(out=cosw[:, :, a, :], in0=cost[:, :, :], scalar=scale,
                                           in1=normw[:, a, None, :].to_broadcast([P, TPB, D]), op0=ALU.mult, op1=ALU.mult)
                    for lo, hi in ((0, D // 2), (D // 2, 0)):
                        last = v.scalar_tensor_tensor(
                            out=sinw[:, :, a, lo:lo + D // 2], in0=sint[:, :, lo:lo + D // 2], scalar=scale,
                            in1=normw[:, a, None, hi:hi + D // 2].to_broadcast([P, TPB, D // 2]), op0=ALU.mult, op1=ALU.mult)
                last.then_inc(s_tab, 1)

                with dve.Fori(0, B // 2) as k:
                    for par in range(2):
                        bb = k * 2 + par
                        dve.wait_ge(s_x, bb * 16 + 16)
                        ln_dve(nc, dve, bb, bb, par, x, stats, mv, lnr, lnx, s_mark, s_bn, s_mv, s_lnr, s_lnT, s_lnx)

                for kind, s, b in attention_schedule(dve):
                    if kind == TAIL:
                        dve.wait_ge(s_yt, b + 1)
                        xs = x[:, bass.ds(b * TPB, TPB), :] if not isinstance(b, int) else x[:, b * TPB:(b + 1) * TPB, :]
                        v.tensor_tensor(out=xs, in0=xs, in1=bank_m[:, :].rearrange("p (t c) -> p t c", c=C),
                                        op=ALU.add).then_inc(s_x2, 1)
                        continue
                    n = number_of(s)
                    for q in range(4):
                        if has_tile(s, q, 1):
                            r = (q - 1) % 4
                            wait(dve, s_exp, n * 4 + q)
                            v.reciprocal(rinv[:, r, :], psums[:, r, :]).then_inc(s_rinv, 1)
                            wait(dve, s_rinv, n * 4 + q)
                            for h in range(2):
                                last = v.tensor_scalar(prob_tile(h, r), prob_tile(h, r), rinv[:, r, h:h + 1], None,
                                                       ALU.mult)
                            last.then_inc(s_norm, 1)
                        if has_unit(s, 0):
                            wait(dve, s_scores, n * 4 + (q + 1))
                            v.tensor_reduce(out=negm[:, q, :], in_=bank_s[:, q % 2, :, 0:(q + 1) * P], axis=AX.X,
                                            op=ALU.max, negate=True).then_inc(s_negm, 1)
                        if q == 0 and has_unit(s, 1):
                            wait(dve, s_sq, n + 2)
                            v.tensor_reduce(out=ss[:, :], in_=qk_heads(sq), axis=AX.X, op=ALU.add).then_inc(s_ss, 1)
                        if q == 1 and has_unit(s, 1):
                            wait(dve, s_rstd, n + 2)
                            up = (parity_of(s) + 1) % 2
                            v.tensor_tensor(
                                out=qk_heads(sc), in0=raw[:, up, :, 0:2 * P].rearrange("p t (a d) -> p t a d", d=D),
                                in1=rstd[:, :].rearrange("p (t a) -> p t a", a=4)[:, :, :, None].to_broadcast([P, TPB, 4, D]),
                                op=ALU.mult).then_inc(s_sc, 1)
                        if q == 2 and has_unit(s, 1):
                            wait(dve, s_sc, n + 2)
                            v.tensor_tensor(out=by_head(rot), in0=by_head(sc),
                                            in1=table(cosw)[:, :, None, :].to_broadcast([P, 8, 2, D]),
                                            op=ALU.mult).then_inc(s_cos, 1)
                        if q == 3 and has_unit(s, 1):
                            wait(dve, s_cos, n + 2)
                            wait(dve, s_sin, n + 2)
                            v.tensor_tensor(out=rot[:, :, :], in0=rot[:, :, :], in1=swp[:, :, :],
                                            op=ALU.add).then_inc(s_rope, 1)
                        if has_tile(s, q, LAG):
                            r = (q - LAG) % 4
                            wait(dve, s_pt, n * 4 + (q - LAG + 1))
                            v.tensor_copy(
                                probT[:, :, 0:r + 1, r * P:(r + 1) * P],
                                bank_t[:, :, 0:(r + 1) * P].rearrange("p h (j k) -> p h j k", k=P)).then_inc(s_probT, 1)

            @block.scalar
            def _(act):
                a = nc.scalar
                with act.Fori(0, B // 2) as k:
                    for par in range(2):
                        bb = k * 2 + par
                        act.wait_ge(s_lnT, bb + 1)
                        settle(act, s_mark)
                        a.activation(xnT_all[:, bass.ds(bb * TPB, TPB), :],
                                     bank_t[:, par, :].rearrange("p (t k) -> p t k", k=P), ACT.Copy).then_inc(s_xnT, 1)

                for kind, s, b in attention_schedule(act):
                    if kind == TAIL:
                        act.wait_ge(s_y, b + 2)
                        a.activation(yT[:, :], bank_m[:, :], ACT.Copy).then_inc(s_yT, 1)
                        continue
                    n = number_of(s)
                    par = parity_of(s)
                    up = (par + 1) % 2
                    for q in range(4):
                        if q == 0 and has_unit(s, 1):
                            wait(act, s_raw, n * 4 + 8)
                            wait(act, s_ss, n + 1)
                            a.activation(sq[:, :, :], raw[:, up, :, 0:2 * P], ACT.Square).then_inc(s_sq, 1)
                        if q == 3 and has_unit(s, -1):
                            wait(act, s_pv, n)
                            wait(act, s_y, b + 1)
                            settle(act, s_mark)
                            p = pair_before(s)
                            dst = outT[:, p, :] if isinstance(p, int) else \
                                outT[:, bass.ds(p, 1), :].rearrange("p a k -> p (a k)")
                            a.activation(dst, bank_o[:, :], ACT.Copy).then_inc(s_outT, 1)
                        if has_unit(s, 2):
                            wait(act, s_proj, n * 4 + (q + 9))
                            if q == 0:
                                wait(act, s_v[par], n * 8 + (16 - 8 * par))
                                wait(act, s_sc, n + 1)
                            a.activation(raw[:, par, q, :], bank_m[:, 0:QKV], ACT.Copy).then_inc(s_raw, 1)
                        if has_unit(s, 0):
                            wait(act, s_negm, n * 4 + (q + 1))
                            for h in range(2):
                                last = a.activation(prob_tile(h, q), bank_s[:, q % 2, h, 0:(q + 1) * P], ACT.Exp,
                                                    bias=negm[:, q, h:h + 1], accum_out=psums[:, q, h:h + 1])
                            last.then_inc(s_exp, 1)
                        if q == 3 and has_unit(s, 1):
                            for w in range(2):
                                wait(act, s_qkTp, n * 2 + (3 + w))
                                a.activation(qkT[:, up, w, :], bank_m[:, :], ACT.Copy).then_inc(s_qkT, 1)

            @block.tensor
            def _(pe):
                t = nc.tensor
                pe.sem_inc(s_y, 1)
                pe.wait_ge(s_const, 2)
                with pe.Fori(0, B // 2) as k:
                    for par in range(2):
                        bb = k * 2 + par
                        pe.wait_ge(s_lnx, bb + 1)
                        if par == 1:
                            pe.wait_ge(s_xnT, bb)
                        for i in range(TPB):
                            last = t.transpose(bank_t[:, par, i * P:(i + 1) * P], lnx[:, par, i, :], ident[:, :])
                        last.then_inc(s_lnT, 1)

                pe.wait_ge(s_load, 16 * 6)
                for kind, s, b in attention_schedule(pe):
                    if kind == TAIL:
                        pe.wait_ge(s_outT, b * 8 + 8)
                        pe.wait_ge(s_qkT, 2 * UNITS if isinstance(b, int) else b * 16 + 20)
                        for p in range(NP):
                            last = t.matmul(bank_m[:, :], wo[:, p, :], outT[:, p, :], start=(p == 0), stop=(p == NP - 1))
                        last.then_inc(s_y, 1)
                        pe.wait_ge(s_yT, b + 1)
                        for i in range(TPB):
                            last = t.transpose(bank_m[:, i * P:(i + 1) * P], yT[:, i * P:(i + 1) * P], ident[:, :])
                        last.then_inc(s_yt, 1)
                        continue
                    n = number_of(s)
                    par = parity_of(s)
                    up = (par + 1) % 2
                    for q in range(4):
                        if has_unit(s, 0):
                            if q == 0:
                                wait(pe, s_qkT, n * 2 + 2)
                            wait(pe, s_exp, n * 4 + (q - 1))
                            keys = (q + 1) * P
                            for h in range(2):
                                t.matmul(bank_s[:, q % 2, h, 0:keys], qkT[D * h:D * h + D, par, 0, q * P:keys],
                                         qkT[D * h:D * h + D, par, 1, 0:keys], start=True, stop=False,
                                         skip_group_check=True)
                            for h in range(2):
                                last = t.matmul(bank_s[:, q % 2, h, q * P:keys], identb[:, :], causal[:, :],
                                                start=False, stop=True, skip_group_check=True)
                            last.then_inc(s_scores, 1)
                        if has_unit(s, 2):
                            if q == 0:
                                wait(pe, s_w[par], n * 16 + (64 - 16 * par))
                                if isinstance(s, int) and s < 0:
                                    wait(pe, s_raw, 4 * (s + 2))
                                else:
                                    wait(pe, s_qkT, n * 2 + 2)
                                    wait(pe, s_x2, b + 1)
                            else:
                                wait(pe, s_raw, n * 4 + (8 + q))
                            t.matmul(bank_m[:, 0:QKV], xbuf[:, par, q * P:(q + 1) * P], wbuf[:, par, :],
                                     start=True, stop=True).then_inc(s_proj, 1)
                        if q == 2 and has_unit(s, -1):
                            wait(pe, s_probT, n * 4)
                            wait(pe, s_v[up], n * 8 + (8 - 8 * up))
                            for j in range(TPB):
                                for h in range(2):
                                    last = t.matmul(bank_o[D * h:D * h + D, j * P:T], vbuf[:, up, j, D * h:D * h + D],
                                                    probT[:, h, j, j * P:T], start=(j == 0), stop=(j == TPB - 1),
                                                    skip_group_check=True)
                            last.then_inc(s_pv, 1)
                        if has_tile(s, q, LAG):
                            r = (q - LAG) % 4
                            wait(pe, s_norm, n * 4 + (q - LAG + 1))
                            wait(pe, s_probT, n * 4 + (q - LAG))
                            for h in range(2):
                                for j in range(r + 1):
                                    last = t.transpose(bank_t[:, h, j * P:(j + 1) * P],
                                                       prob[:, h, PROB_OFF[r] + j * P:PROB_OFF[r] + (j + 1) * P],
                                                       ident[:, :])
                            last.then_inc(s_pt, 1)
                        if q == 3 and has_unit(s, 1):
                            wait(pe, s_rope, n + 2)
                            for w in range(2):
                                if w:
                                    wait(pe, s_qkT, n * 2 + 3)
                                elif has_unit(s, 2):
                                    wait(pe, s_raw, n * 4 + 12)
                                else:
                                    wait(pe, s_qkT, n * 2 + 2)
                                for i in range(TPB):
                                    last = t.transpose(bank_m[:, i * P:(i + 1) * P], rot[:, i, w * P:(w + 1) * P],
                                                       ident[:, :])
                                last.then_inc(s_qkTp, 1)

        inner.close()
        experts(nc, x, xn2, ident, before, onesb, half, stats, mv, lnv, lnr, lnx, s_mark,
                (s_bn, s_mv, s_lnv, s_lnr, s_lnx, s_lnT, s_fill), out_tiles, packed, expert_out,
                rw_in, rb_in, w1_in, b1_in, w2_in, b2_in, 16 * (SLOTS // zero_rows))


def ln_dve(nc, dve, count, b, par, x, stats, mv, lnr, lnx, s_mark, s_bn, s_mv, s_lnr, s_lnT, s_lnx):
    v = nc.vector
    for i in range(TPB):
        last = v.bn_stats(stats[:, par, i, :], x[:, bass.ds(b * TPB + i, 1), :].rearrange("p a c -> p (a c)"))
    last.then_inc(s_bn, 1)
    dve.wait_ge(s_bn, count + 1)
    settle(dve, s_mark)
    for i in range(TPB):
        last = v.bn_aggr(mv[:, par, i, :], stats[:, par, i, :])
    last.then_inc(s_mv, 1)
    dve.wait_ge(s_lnr, count + 1)
    if par == 1:
        dve.wait_ge(s_lnT, count)
    for i in range(TPB):
        last = v.tensor_scalar(lnx[:, par, i, :], x[:, bass.ds(b * TPB + i, 1), :].rearrange("p a c -> p (a c)"),
                               mv[:, par, i, 0:1], lnr[:, par, i:i + 1], ALU.subtract, ALU.mult)
    last.then_inc(s_lnx, 1)


def ln_pool(nc, pool, count, par, mv, lnv, lnr, half, s_mark, s_mv, s_lnv, s_lnr):
    pool.wait_ge(s_mv, count + 1)
    settle(pool, s_mark)
    nc.gpsimd.tensor_scalar(lnv[:, par, :], mv[:, par, :, 1], 1.0, LN_EPS, ALU.mult, ALU.add).then_inc(s_lnv, 1)
    pool.wait_ge(s_lnv, count + 1)
    nc.gpsimd.tensor_tensor(out=lnr[:, par, :], in0=lnv[:, par, :], in1=half[:, 0:1].to_broadcast([P, TPB]),
                            op=ALU.pow).then_inc(s_lnr, 1)


def experts(nc, x, xn2, ident, before, onesb, half, stats, mv, lnv, lnr, lnx, s_mark, sems, out_tiles,
            packed, expert_out, rw_in, rb_in, w1_in, b1_in, w2_in, b2_in, fill_count):
    s_bn, s_mv, s_lnv, s_lnr, s_lnx, s_lnT, s_fill = sems
    w2_view = w2_in.rearrange("e (c p) n -> p e c n", p=P)
    packed_view = packed.rearrange("(e j p) c -> p e j c", e=E, p=P)
    expert_view = expert_out.rearrange("(e j p) c -> p e j c", e=E, p=P)

    with ExitStack() as ctx:
        def sb(name, shape, dt=F32):
            return ctx.enter_context(nc.sbuf_tensor(name, shape, dt))

        def psum(name, shape, dt=F32):
            return ctx.enter_context(nc.psum_tensor(name, shape, dt))

        def sem(name):
            return ctx.enter_context(nc.semaphore(name))

        rw = sb("rw", [P, E])
        rb = sb("rb", [P, E])
        b1 = sb("b1", [P, E * FC])
        b2 = sb("b2", [P, E, C])
        xn2T = sb("xn2T", [P, 2, TPB, P])
        logits = sb("logits", [P, NT, E])
        iota = sb("iota", [P, NT, E])
        cand = sb("cand", [P, NT, E])
        is_max = sb("is_max", [P, NT, E])
        pick = [sb(f"pick{k}", [P, NT, E]) for k in range(TOPK)]
        either = sb("either", [P, NT, E], BF16)
        total = sb("total", [P, NT, E])
        run_a = sb("run_a", [P, NT, E])
        run_b = sb("run_b", [P, NT, E])
        pos = sb("pos", [P, NT, E])
        top = [sb(f"top{k}", [P, NT]) for k in range(TOPK)]
        first = [sb(f"first{k}", [P, NT]) for k in range(TOPK)]
        place = [sb(f"place{k}", [P, NT]) for k in range(TOPK)]
        kept = [sb(f"kept{k}", [P, NT]) for k in range(TOPK)]
        slot = [sb(f"slot{k}", [P, NT]) for k in range(TOPK)]
        gate = [sb(f"gate{k}", [P, NT]) for k in range(TOPK)]
        tmp = [sb(f"tmp{k}", [P, NT]) for k in range(TOPK)]
        scatter_at = [sb(f"scatter_at{k}", [P, NT], U32) for k in range(TOPK)]
        gather_at = [sb(f"gather_at{k}", [P, NT], U32) for k in range(TOPK)]
        gap = sb("gap", [P, NT])
        egap = sb("egap", [P, NT])
        denom = sb("denom", [P, NT])
        xe = sb("xe", [P, 2, SJ, C])
        w1 = sb("w1", [P, 2, F])
        w2 = sb("w2", [P, 2, FC, C])
        xeT = sb("xeT", [P, 2, CAP])
        hT = sb("hT", [P, 2, FC, CAP])
        ye = sb("ye", [P, 2, SJ, C])
        rows = [sb(f"rows{k}", [P, 2, TPB, C]) for k in range(TOPK)]
        res = sb("res", [P, 2, TPB, C])

        bank_x = psum("bank_x", [P, 2, 512])
        bank_h = psum("bank_h", [P, 2, 2, 512])
        bank_y = psum("bank_y", [P, 2, 512])

        s_load = sem("s_load2")
        s_iota = sem("s_iota")
        s_xn2 = sem("s_xn2")
        s_xn2T = sem("s_xn2T")
        s_lgp = sem("s_lgp")
        s_logits = sem("s_logits")
        s_r = sem("s_r")
        s_either = sem("s_either")
        s_pos = sem("s_pos")
        s_gap = sem("s_gap")
        s_egap = sem("s_egap")
        s_at = sem("s_at")
        s_scat = sem("s_scat")
        s_xe = [sem("s_xe0"), sem("s_xe1")]
        s_w1 = [sem("s_w1_0"), sem("s_w1_1")]
        s_w2 = [sem("s_w2_0"), sem("s_w2_1")]
        s_xTp = sem("s_xTp")
        s_xT = sem("s_xT")
        s_hp = sem("s_hp")
        s_h = sem("s_h")
        s_yp = sem("s_yp")
        s_ye = sem("s_ye")
        s_store = [sem("s_store0"), sem("s_store1")]
        s_rows = [sem("s_rows0"), sem("s_rows1")]
        s_mid = sem("s_mid")
        s_res = sem("s_res")
        s_out = [sem("s_out0"), sem("s_out1")]

        with nc.Block() as block:

            @block.sync
            def _(sp):
                for dst, src in ((rw[:, :], rw_in),
                                 (rb[:, :], rb_in.rearrange("(a n) -> a n", a=1).to_broadcast([P, E])),
                                 (b1[:, :], b1_in),
                                 (b2[:, :, :].rearrange("p e c -> p (e c)"),
                                  b2_in.rearrange("(a e) c -> a (e c)", a=1).to_broadcast([P, E * C]))):
                    sp.dma_start(dst, src).then_inc(s_load, 16)

                def load_slots(e, par):
                    src = packed_view[:, e] if isinstance(e, int) else \
                        packed_view[:, bass.ds(e, 1)].rearrange("p e j c -> p (e j) c")
                    sp.dma_start(xe[:, par, :, :], src).then_inc(s_xe[par], 16)

                def load_w1(e, par):
                    src = w1_in[e] if isinstance(e, int) else w1_in[bass.ds(e, 1)].rearrange("e p f -> p (e f)")
                    sp.dma_start(w1[:, par, :], src).then_inc(s_w1[par], 16)

                def load_w2(e, par):
                    src = w2_view[:, e] if isinstance(e, int) else \
                        w2_view[:, bass.ds(e, 1)].rearrange("p e c n -> p (e c) n")
                    sp.dma_start(w2[:, par, :, :], src).then_inc(s_w2[par], 16)

                def store_expert(e, par):
                    sp.wait_ge(s_ye, e * 2 + 2)
                    settle(sp, s_mark)
                    dst = expert_view[:, e] if isinstance(e, int) else \
                        expert_view[:, bass.ds(e, 1)].rearrange("p e j c -> p (e j) c")
                    sp.dma_start(dst, ye[:, par, :, :]).then_inc(s_store[par], 16)

                for e in range(2):
                    load_w1(e, e)
                    load_w2(e, e)
                sp.wait_ge(s_scat, 16 * TOPK * NT)
                for e in range(2):
                    load_slots(e, e)
                with sp.Fori(0, E // 2 - 1) as k:
                    for par in range(2):
                        e = k * 2 + par
                        sp.wait_ge(s_xTp, e + 1)
                        settle(sp, s_mark)
                        load_slots(e + 2, par)
                        sp.wait_ge(s_hp, e * 8 + 8)
                        settle(sp, s_mark)
                        load_w1(e + 2, par)
                        store_expert(e, par)
                        load_w2(e + 2, par)
                for par in range(2):
                    store_expert(E - 2 + par, par)
                with sp.Fori(0, B // 2) as k:
                    for par in range(2):
                        sp.wait_ge(s_res, k * 2 + (par + 1))
                        settle(sp, s_mark)
                        sp.dma_start(out_tiles[:, bass.ds(k * 2 + par, 1)].rearrange("p b t c -> p (b t) c"),
                                     res[:, par, :, :]).then_inc(s_out[par], 16)
                for par in range(2):
                    sp.wait_ge(s_out[par], 16 * (B // 2))

            @block.gpsimd
            def _(pool):
                g = nc.gpsimd
                g.iota(iota[:, :, :], pattern=[[0, NT], [1, E]], base=-E, channel_multiplier=0,
                       allow_small_or_imprecise_dtypes=True).then_inc(s_iota, 1)
                with pool.Fori(0, B // 2) as k:
                    for par in range(2):
                        ln_pool(nc, pool, k * 2 + (B + par), par, mv, lnv, lnr, half, s_mark, s_mv, s_lnv, s_lnr)
                pool.wait_ge(s_at, 1)
                pool.wait_ge(s_xn2, B)
                pool.wait_ge(s_fill, fill_count)
                for i in range(NT):
                    for k in range(TOPK):
                        g.indirect_dma_start(out=packed, out_offset=bass.IndirectOffsetOnAxis(ap=scatter_at[k][:, i:i + 1], axis=0),
                                             in_=xn2[:, i, :], in_offset=None, bounds_check=SLOTS - 1,
                                             oob_is_err=False).then_inc(s_scat, 16)
                for par in range(2):
                    pool.wait_ge(s_store[par], 16 * (E // 2))
                for b in range(B):
                    if b >= 2:
                        pool.wait_ge(s_res, b - 1)
                    for i in range(TPB):
                        for k in range(TOPK):
                            at = gather_at[k][:, b * TPB + i:b * TPB + i + 1]
                            g.indirect_dma_start(out=rows[k][:, b % 2, i, :], out_offset=None, in_=expert_out,
                                                 in_offset=bass.IndirectOffsetOnAxis(ap=at, axis=0),
                                                 bounds_check=SLOTS - 1, oob_is_err=False).then_inc(s_rows[b % 2], 16)

            @block.vector
            def _(dve):
                v = nc.vector
                steps = [0]

                def then(ins):
                    steps[0] += 1
                    ins.then_inc(s_r, 1)
                    dve.wait_ge(s_r, steps[0])

                dve.wait_ge(s_load, 64)
                with dve.Fori(0, B // 2) as k:
                    for par in range(2):
                        b = k * 2 + par
                        ln_dve(nc, dve, b + B, b, par, x, stats, mv, lnr, lnx, s_mark, s_bn, s_mv, s_lnr, s_lnT, s_lnx)
                        dve.wait_ge(s_lgp, b + 1)
                        v.tensor_tensor(out=logits[:, bass.ds(b * TPB, TPB), :],
                                        in0=bank_y[:, par, 0:TPB * E].rearrange("p (t e) -> p t e", e=E),
                                        in1=rb[:, None, :].to_broadcast([P, TPB, E]), op=ALU.add).then_inc(s_logits, 1)
                dve.wait_ge(s_iota, 1)
                dve.wait_ge(s_logits, B)

                def over_experts(t):
                    return t[:, :, None].to_broadcast([P, NT, E])

                for k in range(TOPK):
                    then(v.tensor_reduce(out=top[k][:, :], in_=logits[:, :, :], axis=AX.X, op=ALU.max))
                    if k == 1:
                        v.tensor_tensor(out=gap[:, :], in0=top[1][:, :], in1=top[0][:, :], op=ALU.subtract).then_inc(s_gap, 1)
                    then(v.tensor_tensor(out=is_max[:, :, :], in0=logits[:, :, :], in1=over_experts(top[k]), op=ALU.is_equal))
                    then(v.tensor_tensor(out=cand[:, :, :], in0=is_max[:, :, :], in1=iota[:, :, :], op=ALU.mult))
                    then(v.tensor_reduce(out=first[k][:, :], in_=cand[:, :, :], axis=AX.X, op=ALU.min))
                    then(v.tensor_tensor(out=pick[k][:, :, :], in0=iota[:, :, :], in1=over_experts(first[k]), op=ALU.is_equal))
                    if k == 0:
                        then(v.scalar_tensor_tensor(out=logits[:, :, :], in0=pick[0][:, :, :], scalar=-3.0e38,
                                                    in1=logits[:, :, :], op0=ALU.mult, op1=ALU.add))
                v.tensor_tensor(out=either[:, :, :], in0=pick[0][:, :, :], in1=pick[1][:, :, :], op=ALU.add).then_inc(s_either, 1)

                dve.wait_ge(s_pos, 1)
                then(v.tensor_copy(total[:, :, :], bank_h[:, 0, 1, :].rearrange("p (t e) -> p t e", e=E)))
                then(v.tensor_copy(run_a[:, :, :], total[:, :, :]))
                src, dst, d = run_a, run_b, 1
                while d < NT:
                    then(v.tensor_tensor(out=dst[:, d:, :], in0=src[:, d:, :], in1=src[:, :NT - d, :], op=ALU.add))
                    then(v.tensor_copy(dst[:, :d, :], src[:, :d, :]))
                    src, dst, d = dst, src, 2 * d
                then(v.tensor_tensor(out=dst[:, :, :], in0=src[:, :, :], in1=total[:, :, :], op=ALU.subtract))
                then(v.tensor_tensor(out=pos[:, :, :], in0=dst[:, :, :],
                                     in1=bank_h[:, 0, 0, :].rearrange("p (t e) -> p t e", e=E), op=ALU.add))
                for k in range(TOPK):
                    then(v.tensor_tensor(out=cand[:, :, :], in0=pick[k][:, :, :], in1=pos[:, :, :], op=ALU.mult))
                    then(v.tensor_reduce(out=place[k][:, :], in_=cand[:, :, :], axis=AX.X, op=ALU.add))
                    then(v.tensor_scalar(slot[k][:, :], first[k][:, :], float(CAP), float(SLOTS), ALU.mult, ALU.add))
                    then(v.tensor_tensor(out=slot[k][:, :], in0=slot[k][:, :], in1=place[k][:, :], op=ALU.add))
                    then(v.tensor_scalar(kept[k][:, :], place[k][:, :], float(CAP), None, ALU.is_lt))
                    then(v.tensor_scalar(tmp[k][:, :], kept[k][:, :], float(-2 * SLOTS), float(2 * SLOTS), ALU.mult, ALU.add))
                    then(v.tensor_tensor(out=scatter_at[k][:, :], in0=slot[k][:, :], in1=tmp[k][:, :], op=ALU.add))
                    then(v.tensor_scalar(gather_at[k][:, :], slot[k][:, :], float(SLOTS - 1), None, ALU.min))
                v.tensor_copy(tmp[0][:, :], kept[0][:, :]).then_inc(s_at, 1)

                dve.wait_ge(s_egap, 1)
                dve.wait_ge(s_at, 1)
                then(v.tensor_scalar(denom[:, :], egap[:, :], 1.0, None, ALU.add))
                then(v.reciprocal(gate[0][:, :], denom[:, :]))
                then(v.tensor_tensor(out=gate[1][:, :], in0=gate[0][:, :], in1=egap[:, :], op=ALU.mult))
                for k in range(TOPK):
                    then(v.tensor_tensor(out=tmp[k][:, :], in0=gate[k][:, :], in1=kept[k][:, :], op=ALU.mult))
                then(v.tensor_tensor(out=denom[:, :], in0=tmp[0][:, :], in1=tmp[1][:, :], op=ALU.add))
                then(v.tensor_scalar(denom[:, :], denom[:, :], 1e-9, None, ALU.add))
                then(v.reciprocal(gap[:, :], denom[:, :]))
                for k in range(TOPK):
                    then(v.tensor_tensor(out=gate[k][:, :], in0=tmp[k][:, :], in1=gap[:, :], op=ALU.mult))

                def add_bias(e, par):
                    bias = b2[:, e, :] if isinstance(e, int) else b2[:, bass.ds(e, 1), :].rearrange("p a c -> p (a c)")
                    wait(dve, s_store[par], e * 8 - 8 * par)
                    for part, (lo, n) in enumerate(((0, 4), (4, 1))):
                        dve.wait_ge(s_yp, e * 2 + (part + 1))
                        v.tensor_tensor(out=ye[:, par, lo:lo + n, :],
                                        in0=bank_y[:, part, 0:n * C].rearrange("p (j c) -> p j c", c=C),
                                        in1=bias[:, None, :].to_broadcast([P, n, C]), op=ALU.add).then_inc(s_ye, 1)

                def slots_out(e, par):
                    dve.wait_ge(s_xTp, e + 1)
                    v.tensor_copy(xeT[:, par, 0:512], bank_x[:, 0, :])
                    v.tensor_copy(xeT[:, par, 512:CAP], bank_x[:, 1, 0:CAP - 512]).then_inc(s_xT, 1)

                slots_out(0, 0)
                slots_out(1, 1)
                for par in range(2):
                    slots_out(2 + par, par)
                    add_bias(par, par)
                with dve.Fori(1, E // 2 - 1) as k:
                    for par in range(2):
                        slots_out(k * 2 + (2 + par), par)
                        add_bias(k * 2 + par, par)
                for par in range(2):
                    add_bias(E - 2 + par, par)

                def combine(k, par):
                    dve.wait_ge(s_rows[par], k * (16 * TPB * TOPK) + 16 * TPB * TOPK)
                    wait(dve, s_out[par], k * 16)

                    def column(t, i):
                        n = k * (2 * TPB) + (par * TPB + i)
                        return t[:, n:n + 1] if isinstance(n, int) else t[:, bass.ds(n, 1)]

                    for i in range(TPB):
                        last = v.scalar_tensor_tensor(
                            out=res[:, par, i, :], in0=rows[0][:, par, i, :], scalar=column(gate[0], i),
                            in1=column(x, i).rearrange("p a c -> p (a c)"), op0=ALU.mult, op1=ALU.add)
                    last.then_inc(s_mid, 1)
                    dve.wait_ge(s_mid, k * 2 + (par + 1))
                    for i in range(TPB):
                        last = v.scalar_tensor_tensor(
                            out=res[:, par, i, :], in0=rows[1][:, par, i, :], scalar=column(gate[1], i),
                            in1=res[:, par, i, :], op0=ALU.mult, op1=ALU.add)
                    last.then_inc(s_res, 1)

                for par in range(2):
                    combine(0, par)
                with dve.Fori(1, B // 2) as k:
                    for par in range(2):
                        combine(k, par)

            @block.scalar
            def _(act):
                a = nc.scalar
                with act.Fori(0, B // 2) as k:
                    for par in range(2):
                        b = k * 2 + par
                        act.wait_ge(s_lnT, b + (B + 1))
                        a.activation(xn2T[:, par, :, :], bank_x[:, par, :].rearrange("p (t k) -> p t k", k=P),
                                     ACT.Copy).then_inc(s_xn2T, 1)
                        a.activation(xn2[:, bass.ds(b * TPB, TPB), :], lnx[:, par, :, :], ACT.Copy).then_inc(s_xn2, 1)
                act.wait_ge(s_gap, 1)
                a.activation(egap[:, :], gap[:, :], ACT.Exp).then_inc(s_egap, 1)
                act.wait_ge(s_load, 64)
                with act.Fori(0, E // 2) as k:
                    for par in range(2):
                        e = k * 2 + par
                        for c in range(FC):
                            for hf in range(2):
                                act.wait_ge(s_hp, e * 8 + (2 * c + hf + 1))
                                settle(act, s_mark)
                                a.activation(hT[:, par, c, hf * HALF:(hf + 1) * HALF], bank_h[:, c % 2, hf, 0:HALF],
                                             ACT.Gelu, bias=b1[:, bass.ds(e * FC + c, 1)]).then_inc(s_h, 1)

            @block.tensor
            def _(pe):
                t = nc.tensor
                pe.wait_ge(s_load, 64)
                with pe.Fori(0, B // 2) as k:
                    for par in range(2):
                        b = k * 2 + par
                        pe.wait_ge(s_lnx, b + (B + 1))
                        for i in range(TPB):
                            last = t.transpose(bank_x[:, par, i * P:(i + 1) * P], lnx[:, par, i, :], ident[:, :])
                        last.then_inc(s_lnT, 1)
                        pe.wait_ge(s_xn2T, b + 1)
                        if par == 1:
                            pe.wait_ge(s_logits, b)
                        for i in range(TPB):
                            last = t.matmul(bank_y[:, par, i * E:(i + 1) * E], xn2T[:, par, i, :], rw[:, :], start=True, stop=True)
                        last.then_inc(s_lgp, 1)
                pe.wait_ge(s_either, 1)
                t.matmul(bank_h[:, 0, 0, :], before[:, :], either[:, :, :].rearrange("p t e -> p (t e)"), start=True, stop=True)
                t.matmul(bank_h[:, 0, 1, :], onesb[:, :], either[:, :, :].rearrange("p t e -> p (t e)"),
                         start=True, stop=True).then_inc(s_pos, 1)

                def slots_in(e, par):
                    pe.wait_ge(s_xe[par], e * 8 + (16 - 8 * par))
                    wait(pe, s_xT, e)
                    for j in range(SJ):
                        last = t.transpose(bank_x[:, j // 4, (j % 4) * P:(j % 4 + 1) * P], xe[:, par, j, :], ident[:, :])
                    last.then_inc(s_xTp, 1)

                def hidden(e, par):
                    pe.wait_ge(s_xT, e + 1)
                    pe.wait_ge(s_w1[par], e * 8 + (16 - 8 * par))
                    for c in range(FC):
                        for hf in range(2):
                            wait(pe, s_h, e * 8 + (2 * c + hf - 3))
                            t.matmul(bank_h[:, c % 2, hf, 0:HALF], w1[:, par, c * P:(c + 1) * P],
                                     xeT[:, par, hf * HALF:(hf + 1) * HALF], start=True, stop=True).then_inc(s_hp, 1)

                def outputs(e, par):
                    pe.wait_ge(s_h, e * 8 + 8)
                    pe.wait_ge(s_w2[par], e * 8 + (16 - 8 * par))
                    wait(pe, s_ye, e * 2)
                    for j in range(SJ):
                        for c in range(FC):
                            last = t.matmul(bank_y[:, j // 4, (j % 4) * C:(j % 4 + 1) * C], hT[:, par, c, j * P:(j + 1) * P],
                                            w2[:, par, c, :], start=(c == 0), stop=(c == FC - 1))
                        if j >= 3:
                            last.then_inc(s_yp, 1)

                slots_in(0, 0)
                hidden(0, 0)
                slots_in(1, 1)
                with pe.Fori(0, E // 2 - 1) as k:
                    for e, par in ((k * 2 + 1, 1), (k * 2 + 2, 0)):
                        hidden(e, par)
                        slots_in(e + 1, 1 - par)
                        outputs(e - 1, 1 - par)
                hidden(E - 1, 1)
                outputs(E - 2, 0)
                outputs(E - 1, 1)


def rope_tables():
    import numpy as np
    inv_freq = np.float32(1.0) / np.float32(10000.0) ** (np.arange(0, D, 2, dtype=np.float32) / np.float32(D))
    angle = np.arange(T, dtype=np.float32)[:, None] * inv_freq
    cos, sin = np.cos(angle), np.sin(angle)

    def tiles(a):
        return np.ascontiguousarray(a.reshape(TPB, P, D).transpose(1, 0, 2)).astype(np.float32)

    return tiles(np.concatenate([cos, cos], axis=1)), tiles(np.concatenate([-sin, sin], axis=1))


def kernel(L0_attn_x, L0_attn_wqkv, L0_attn_wo, L0_attn_q_norm_w, L0_attn_k_norm_w, L0_ffn_router_w,
           L0_ffn_router_b, L0_ffn_w1, L0_ffn_b1, L0_ffn_w2, L0_ffn_b2):
    import numpy as np
    import concourse.bacc as bacc
    from concourse.bass_utils import run_bass_kernel_spmd

    cos, sin = rope_tables()
    laid = {
        "x": np.ascontiguousarray(L0_attn_x),
        "wqkv": np.ascontiguousarray(np.asarray(L0_attn_wqkv).reshape(3, NP, P, C).transpose(3, 1, 0, 2).reshape(C, NP, QKV)),
        "wo": np.ascontiguousarray(np.asarray(L0_attn_wo).reshape(C, NP, P).transpose(2, 1, 0)),
        "q_norm_w": np.ascontiguousarray(L0_attn_q_norm_w),
        "k_norm_w": np.ascontiguousarray(L0_attn_k_norm_w),
        "router_w": np.ascontiguousarray(np.asarray(L0_ffn_router_w).T),
        "router_b": np.ascontiguousarray(L0_ffn_router_b),
        "w1": np.ascontiguousarray(L0_ffn_w1),
        "b1": np.ascontiguousarray(np.asarray(L0_ffn_b1).reshape(E * FC, P).T),
        "w2": np.ascontiguousarray(L0_ffn_w2),
        "b2": np.ascontiguousarray(L0_ffn_b2),
        "cos": cos,
        "sin": sin,
    }
    nc = bacc.Bacc("TRN2", target_bir_lowering=False, num_devices=1)
    args = [nc.dram_tensor(f"in_{n}", a.shape, mybir.dt.from_np(a.dtype), kind="ExternalInput").ap() for n, a in laid.items()]
    out = nc.dram_tensor("out_0", (B, T, C), F32, kind="ExternalOutput").ap()
    build(nc, *args, out)
    r = run_bass_kernel_spmd(nc, [{f"in_{n}": a for n, a in laid.items()}], core_ids=[0])
    return r.results[0]["out_0"]
```

```python
import concourse.bass as bass
from concourse import mybir
from contextlib import ExitStack

F32 = mybir.dt.float32
BF16 = mybir.dt.bfloat16
U32 = mybir.dt.uint32
ALU = mybir.AluOpType
ACT = mybir.ActivationFunctionType
AX = mybir.AxisListType

P = 128
B, T, C = 8, 512, 128
H, D = 16, 64
TPB = T // P
NT = B * TPB
NP = H // 2
UNITS = B * NP
QKV = 3 * P
E, F, TOPK = 16, 512, 2
FC = F // P
CAP = -(-5 * B * T * TOPK // (4 * E))
SJ = CAP // P
HALF = CAP // 2
SLOTS = E * CAP
RMS_EPS, LN_EPS = 1e-6, 1e-5
MASKED = -1e30
LOADS = 4
LAG = 2
PROB_OFF = [P * q * (q + 1) // 2 for q in range(TPB)]
PROB_COLS = P * TPB * (TPB + 1) // 2

PLAIN, PROJECT_OUT, ROUTE = "plain", "project_out", "route"


class Step:

    def __init__(self, number, parity, pair_before, batch, extra=PLAIN):
        self.number, self.parity, self.pair_before = number, parity, pair_before
        self.batch, self.extra = batch, extra


def attention_steps(eng):
    for s in range(-2, 3):
        yield Step(s, s % 2, (s - 1) % NP, 0)
    with eng.Fori(0, B - 1) as b:
        with eng.Fori(0, NP // 2 - 1) as it:
            for k in range(2):
                yield Step(b * 8 + it * 2 + (3 + k), (1 + k) % 2, it * 2 + (2 + k), b)
        yield Step(b * 8 + 9, 1, 0, b, PROJECT_OUT)
        yield Step(b * 8 + 10, 0, 1, b, ROUTE)
    for s in range(UNITS - 5, UNITS + 1):
        yield Step(s, s % 2, (s - 1) % NP, B - 1)


def has_unit(step, offset):
    return not isinstance(step.number, int) or 0 <= step.number + offset < UNITS


def has_tile(step, q, lag):
    return not isinstance(step.number, int) or 0 <= 4 * step.number + q - lag < 4 * UNITS


def tiles_of(t, batch):
    if isinstance(batch, int):
        return t[:, batch * TPB:(batch + 1) * TPB]
    return t[:, bass.ds(batch * TPB, TPB)]


def settle(eng, s_mark):
    eng.sem_inc(s_mark, 1)


def wait(eng, sem, value):
    if isinstance(value, int) and value <= 0:
        return
    eng.wait_ge(sem, value)


def build(nc, x_in, wqkv_in, wo_in, qw_in, kw_in, rw_in, rb_in, w1_in, b1_in, w2_in, b2_in, cos_in, sin_in, out):
    packed = nc.dram_tensor("packed", (SLOTS, C), F32, kind="Internal").ap()
    expert_out = nc.dram_tensor("expert_out", (SLOTS, C), F32, kind="Internal").ap()
    zero_rows = P * PROB_COLS * 2 // C
    x_tiles = x_in.rearrange("b (t p) c -> p b t c", p=P)
    out_tiles = out.rearrange("b (t p) c -> p b t c", p=P)

    with ExitStack() as ctx:
        def sb(name, shape, dt=F32):
            return ctx.enter_context(nc.sbuf_tensor(name, shape, dt))

        def psum(name, shape, dt=F32):
            return inner.enter_context(nc.psum_tensor(name, shape, dt))

        def sem(name):
            return ctx.enter_context(nc.semaphore(name))

        inner = ctx.enter_context(ExitStack())

        def sba(name, shape, dt=F32):
            return inner.enter_context(nc.sbuf_tensor(name, shape, dt))

        x = sb("x", [P, NT, C])
        xnT_all = sb("xnT_all", [P, NT, P])
        xn2 = sb("xn2", [P, NT, C])
        logits = sb("logits", [P, NT, E])
        ident = sb("ident", [P, P])
        identb = sb("identb", [P, P], BF16)
        before = sb("before", [P, P], BF16)
        onesb = sb("onesb", [P, P], BF16)
        half = sb("half", [P, 1])
        stats = sb("stats", [P, 2, TPB, 6])
        mv = sb("mv", [P, 2, TPB, 2])
        lnv = sb("lnv", [P, 2, TPB])
        lnr = sb("lnr", [P, 2, TPB])
        lnx = sb("lnx", [P, 2, TPB, C])
        wqkv = sba("wqkv", [P, NP, QKV])
        wo = sba("wo", [P, NP, C])
        causal = sba("causal", [P, P], BF16)
        normw = sba("normw", [P, 2, D])
        cosw = sba("cosw", [P, TPB, 2, D])
        sinw = sba("sinw", [P, TPB, 2, D])
        cost = sba("cost", [P, TPB, D])
        sint = sba("sint", [P, TPB, D])
        wbuf = sba("wbuf", [P, 2, QKV])
        xbuf = sba("xbuf", [P, 2, T])
        raw = sba("raw", [P, 2, TPB, QKV])
        vbuf = sba("vbuf", [P, 2, TPB, P])
        sq = sba("sq", [P, TPB, 2 * P])
        ss = sba("ss", [P, TPB * 4])
        ssv = sba("ssv", [P, TPB * 4])
        rstd = sba("rstd", [P, TPB * 4])
        sc = sba("sc", [P, TPB, 2 * P])
        rot = sba("rot", [P, TPB, 2 * P])
        swp = sba("swp", [P, TPB, 2 * P])
        qkT = sba("qkT", [P, 2, 2, T])
        negm = sba("negm", [P, TPB, 2])
        psums = sba("psums", [P, TPB, 2])
        rinv = sba("rinv", [P, TPB, 2])
        prob = sba("prob", [P, 2, PROB_COLS])
        probT = sba("probT", [P, 2, TPB, T])
        outT = sba("outT", [P, NP, T])
        yT = sba("yT", [P, T])
        rw = sba("rw", [P, E])
        rb = sba("rb", [P, E])
        eps = sba("eps", [P, 2])
        xn2T = sba("xn2T", [P, TPB, P])

        bank_s = psum("bank_s", [P, 2, 2, 512])
        bank_t = psum("bank_t", [P, 2, 512])
        bank_o = psum("bank_o", [P, 512])
        bank_m = psum("bank_m", [P, 512])

        s_load = sem("s_load")
        s_tables = sem("s_tables")
        s_x = sem("s_x")
        s_const = sem("s_const")
        s_mark = sem("s_mark")
        s_tab = sem("s_tab")
        s_bn = sem("s_bn")
        s_mv = sem("s_mv")
        s_lnv = sem("s_lnv")
        s_lnr = sem("s_lnr")
        s_lnx = sem("s_lnx")
        s_lnT = sem("s_lnT")
        s_xnT = sem("s_xnT")
        s_w = [sem("s_w0"), sem("s_w1")]
        s_proj = sem("s_proj")
        s_raw = sem("s_raw")
        s_probA = sem("s_probA")
        s_xn2 = sem("s_xn2")
        s_xn2T = sem("s_xn2T")
        s_router = sem("s_router")
        s_logits = sem("s_logits")
        s_v = [sem("s_v0"), sem("s_v1")]
        s_sq = sem("s_sq")
        s_ss = sem("s_ss")
        s_ssv = sem("s_ssv")
        s_rstd = sem("s_rstd")
        s_sc = sem("s_sc")
        s_cos = sem("s_cos")
        s_sin = sem("s_sin")
        s_rope = sem("s_rope")
        s_qkTp = sem("s_qkTp")
        s_qkT = sem("s_qkT")
        s_scores = sem("s_scores")
        s_negm = sem("s_negm")
        s_exp = sem("s_exp")
        s_rinv = sem("s_rinv")
        s_norm = sem("s_norm")
        s_pt = sem("s_pt")
        s_probT = sem("s_probT")
        s_pv = sem("s_pv")
        s_outT = sem("s_outT")
        s_y = sem("s_y")
        s_yT = sem("s_yT")
        s_yt = sem("s_yt")
        s_x2 = sem("s_x2")
        s_zero = sem("s_zero")
        s_fill = sem("s_fill")

        def qk_heads(t):
            return t[:, :, :].rearrange("p t (a d) -> p t a d", d=D)

        def by_head(t):
            return t[:, :, :].rearrange("p t (a h d) -> p (t a) h d", a=2, h=2)

        def table(t):
            return t[:, :, :, :].rearrange("p t a d -> p (t a) d")

        def prob_tile(h, q):
            return prob[:, h, PROB_OFF[q]:PROB_OFF[q] + (q + 1) * P]

        with nc.Block() as block:

            @block.sync
            def _(sp):
                sp.dma_start(x[:, 0:TPB, :], x_tiles[:, 0, :, :]).then_inc(s_x, 16)
                for dst, src in ((cost[:, :, :], cos_in), (sint[:, :, :], sin_in),
                                 (normw[:, 0, :], qw_in.rearrange("(a d) -> a d", a=1).to_broadcast([P, D])),
                                 (normw[:, 1, :], kw_in.rearrange("(a d) -> a d", a=1).to_broadcast([P, D]))):
                    sp.dma_start(dst, src).then_inc(s_tables, 16)
                for dst, src in ((wqkv[:, :, :], wqkv_in), (wo[:, :, :], wo_in), (rw[:, :], rw_in),
                                 (rb[:, :], rb_in.rearrange("(a n) -> a n", a=1).to_broadcast([P, E]))):
                    sp.dma_start(dst, src).then_inc(s_load, 16)
                with sp.Fori(1, B) as b:
                    sp.wait_ge(s_x, b * 16)
                    settle(sp, s_mark)
                    sp.dma_start(x[:, bass.ds(b * TPB, TPB), :],
                                 x_tiles[:, bass.ds(b, 1), :, :].rearrange("p b t c -> p (b t) c")).then_inc(s_x, 16)
                sp.wait_ge(s_zero, 1)
                for r in range(SLOTS // zero_rows):
                    sp.dma_start(packed[r * zero_rows:(r + 1) * zero_rows, :].rearrange("(p r) c -> p (r c)", p=P),
                                 prob[:, :, :].rearrange("p h n -> p (h n)")).then_inc(s_fill, 16)
                sp.wait_ge(s_fill, 16 * (SLOTS // zero_rows))
                sp.wait_ge(s_load, 16 * LOADS)

                def operands(b, p):
                    sp.wait_ge(s_xnT, b + 1)
                    sp.dma_start(wbuf[:, p % 2, :], wqkv[:, p, :]).then_inc(s_w[p % 2], 16)
                    xn = xnT_all[:, bass.ds(b * TPB, TPB), :] if not isinstance(b, int) else \
                        xnT_all[:, b * TPB:(b + 1) * TPB, :]
                    sp.dma_start(xbuf[:, p % 2, :], xn.rearrange("p t k -> p (t k)")).then_inc(s_w[p % 2], 16)

                def values(u, p):
                    wait(sp, s_raw, u * 4 + 4)
                    wait(sp, s_pv, u)
                    sp.dma_start(vbuf[:, p % 2, :, :], raw[:, p % 2, :, 2 * P:QKV]).then_inc(s_v[p % 2], 16)

                operands(0, 0)
                operands(0, 1)
                values(0, 0)
                sp.wait_ge(s_proj, 4)
                operands(0, 2)
                with sp.Fori(0, B - 1) as b:
                    for p in range(1, NP + 1):
                        values(b * NP + p, p)
                        sp.wait_ge(s_proj, b * (4 * NP) + (4 * p + 4))
                        settle(sp, s_mark)
                        operands(b if p + 2 < NP else b + 1, (p + 2) % NP)
                for p in range(1, NP):
                    values((B - 1) * NP + p, p)
                    if p + 2 < NP:
                        sp.wait_ge(s_proj, 4 * ((B - 1) * NP + p) + 4)
                        operands(B - 1, p + 2)

            @block.gpsimd
            def _(pool):
                g = nc.gpsimd
                g.memset(ident[:, :], 0.0)
                g.memset(identb[:, :], 0.0)
                g.memset(causal[:, :], 0.0)
                g.memset(half[:, :], -0.5)
                g.memset(eps[:, 0:1], RMS_EPS)
                g.memset(eps[:, 1:2], LN_EPS)
                g.memset(before[:, :], 1.0)
                g.memset(onesb[:, :], 1.0).then_inc(s_const, 1)
                pool.wait_ge(s_const, 1)
                for m in (ident, identb):
                    g.affine_select(out=m[:, :], in_=m[:, :], compare_op=ALU.not_equal, fill=1.0, base=0,
                                    pattern=[[-1, P]], channel_multiplier=1)
                g.affine_select(out=causal[:, :], in_=causal[:, :], compare_op=ALU.is_ge, fill=MASKED, base=0,
                                pattern=[[-1, P]], channel_multiplier=1)
                g.affine_select(out=before[:, :], in_=before[:, :], compare_op=ALU.is_gt, fill=0.0, base=0,
                                pattern=[[1, P]], channel_multiplier=-1).then_inc(s_const, 1)
                pool.wait_ge(s_const, 2)

                def ln_rstd(count, par):
                    pool.wait_ge(s_mv, count + 1)
                    g.tensor_tensor(out=lnv[:, par, :], in0=mv[:, par, :, 1], in1=eps[:, 1:2].to_broadcast([P, TPB]),
                                    op=ALU.add).then_inc(s_lnv, 1)
                    pool.wait_ge(s_lnv, count + 1)
                    g.tensor_tensor(out=lnr[:, par, :], in0=lnv[:, par, :], in1=half[:, 0:1].to_broadcast([P, TPB]),
                                    op=ALU.pow).then_inc(s_lnr, 1)

                for par in range(2):
                    ln_rstd(par, par)
                g.memset(prob[:, :, :], 0.0).then_inc(s_zero, 1)
                with pool.Fori(1, B // 2) as k:
                    for par in range(2):
                        ln_rstd(k * 2 + par, par)

                for step in attention_steps(pool):
                    n = step.number
                    if has_unit(step, 1):
                        wait(pool, s_sin, n + 2)
                        wait(pool, s_cos, n + 2)
                        g.tensor_tensor(out=rot[:, :, :], in0=rot[:, :, :], in1=swp[:, :, :], op=ALU.add).then_inc(s_rope, 1)
                    if step.extra == ROUTE:
                        ln_rstd(step.batch + B, 0)
                    if has_unit(step, 2):
                        wait(pool, s_ss, n + 3)
                        g.tensor_tensor(out=ssv[:, :], in0=ss[:, :], in1=eps[:, 0:1].to_broadcast([P, 16]),
                                        op=ALU.add).then_inc(s_ssv, 1)
                        wait(pool, s_ssv, n + 3)
                        g.tensor_tensor(out=rstd[:, :], in0=ssv[:, :], in1=half[:, 0:1].to_broadcast([P, 16]),
                                        op=ALU.pow).then_inc(s_rstd, 1)
                        wait(pool, s_sc, n + 3)
                        src, dst, tab = by_head(sc), by_head(swp), table(sinw)
                        for lo, hi in ((0, D // 2), (D // 2, 0)):
                            last = g.tensor_tensor(
                                out=dst[:, :, :, lo:lo + D // 2], in0=src[:, :, :, hi:hi + D // 2],
                                in1=tab[:, :, None, lo:lo + D // 2].to_broadcast([P, 8, 2, D // 2]), op=ALU.mult)
                        last.then_inc(s_sin, 1)
                ln_rstd(2 * B - 1, 0)

            @block.vector
            def _(dve):
                v = nc.vector
                dve.sem_inc(s_x2, 1)
                dve.sem_inc(s_logits, 1)

                def ln_stats(count, b, par):
                    for i in range(TPB):
                        last = v.bn_stats(stats[:, par, i, :], row(b, i))
                    last.then_inc(s_bn, 1)
                    dve.wait_ge(s_bn, count + 1)
                    settle(dve, s_mark)
                    for i in range(TPB):
                        last = v.bn_aggr(mv[:, par, i, :], stats[:, par, i, :])
                    last.then_inc(s_mv, 1)

                def ln_apply(count, b, par):
                    dve.wait_ge(s_lnr, count + 1)
                    for i in range(TPB):
                        last = v.tensor_scalar(lnx[:, par, i, :], row(b, i), mv[:, par, i, 0:1], lnr[:, par, i:i + 1],
                                               ALU.subtract, ALU.mult)
                    last.then_inc(s_lnx, 1)

                def row(b, i):
                    if isinstance(b, int):
                        return x[:, b * TPB + i, :]
                    return x[:, bass.ds(b * TPB + i, 1), :].rearrange("p a c -> p (a c)")

                for par in range(2):
                    dve.wait_ge(s_x, 16 * par + 16)
                    ln_stats(par, par, par)
                    ln_apply(par, par, par)

                dve.wait_ge(s_tables, 16 * 4)
                for a in range(2):
                    scale = D ** -0.5 if a == 0 else 1.0
                    v.scalar_tensor_tensor(out=cosw[:, :, a, :], in0=cost[:, :, :], scalar=scale,
                                           in1=normw[:, a, None, :].to_broadcast([P, TPB, D]), op0=ALU.mult, op1=ALU.mult)
                    for lo, hi in ((0, D // 2), (D // 2, 0)):
                        last = v.scalar_tensor_tensor(
                            out=sinw[:, :, a, lo:lo + D // 2], in0=sint[:, :, lo:lo + D // 2], scalar=scale,
                            in1=normw[:, a, None, hi:hi + D // 2].to_broadcast([P, TPB, D // 2]), op0=ALU.mult, op1=ALU.mult)
                last.then_inc(s_tab, 1)
                dve.wait_ge(s_tab, 1)

                with dve.Fori(1, B // 2) as k:
                    for par in range(2):
                        b = k * 2 + par
                        dve.wait_ge(s_x, b * 16 + 16)
                        settle(dve, s_mark)
                        ln_stats(b, b, par)
                        dve.wait_ge(s_lnT, b - 1)
                        ln_apply(b, b, par)

                def project_out(b):
                    dve.wait_ge(s_yt, b + 1)
                    v.tensor_tensor(out=tiles_of(x, b), in0=tiles_of(x, b),
                                    in1=bank_m[:, :].rearrange("p (t c) -> p t c", c=C), op=ALU.add).then_inc(s_x2, 1)

                def add_router_bias(b):
                    dve.wait_ge(s_router, b + 1)
                    v.tensor_tensor(out=tiles_of(logits, b), in0=bank_m[:, 0:TPB * E].rearrange("p (t e) -> p t e", e=E),
                                    in1=rb[:, None, :].to_broadcast([P, TPB, E]), op=ALU.add).then_inc(s_logits, 1)

                for step in attention_steps(dve):
                    n, b = step.number, step.batch
                    for q in range(4):
                        if has_tile(step, q, 1):
                            r = (q - 1) % 4
                            wait(dve, s_exp, n * 4 + q)
                            v.reciprocal(rinv[:, r, :], psums[:, r, :]).then_inc(s_rinv, 1)
                            wait(dve, s_rinv, n * 4 + q)
                            for h in range(2):
                                last = v.tensor_scalar(prob_tile(h, r), prob_tile(h, r), rinv[:, r, h:h + 1], None,
                                                       ALU.mult)
                            last.then_inc(s_norm, 1)
                        if has_unit(step, 0):
                            wait(dve, s_scores, n * 4 + (q + 1))
                            v.tensor_reduce(out=negm[:, q, :], in_=bank_s[:, q % 2, :, 0:(q + 1) * P], axis=AX.X,
                                            op=ALU.max, negate=True).then_inc(s_negm, 1)
                        if q == 0 and has_unit(step, 1):
                            wait(dve, s_sc, n + 2)
                            wait(dve, s_qkTp, n * 2 + 2)
                            v.tensor_tensor(out=by_head(rot), in0=by_head(sc),
                                            in1=table(cosw)[:, :, None, :].to_broadcast([P, 8, 2, D]),
                                            op=ALU.mult).then_inc(s_cos, 1)
                        if q == 2 and has_unit(step, 2):
                            wait(dve, s_sq, n + 3)
                            v.tensor_reduce(out=ss[:, :], in_=qk_heads(sq), axis=AX.X, op=ALU.add).then_inc(s_ss, 1)
                        if (q - LAG) % 4 != 3 and has_tile(step, q, LAG):
                            r = (q - LAG) % 4
                            wait(dve, s_pt, n * 4 + (q - LAG + 1))
                            v.tensor_copy(
                                probT[:, :, 0:r + 1, r * P:(r + 1) * P],
                                bank_t[:, :, 0:(r + 1) * P].rearrange("p h (j k) -> p h j k", k=P)).then_inc(s_probT, 1)
                        if q == 3 and has_unit(step, 2):
                            wait(dve, s_rstd, n + 3)
                            wait(dve, s_sin, n + 2)
                            v.tensor_tensor(
                                out=qk_heads(sc), in0=raw[:, step.parity, :, 0:2 * P].rearrange("p t (a d) -> p t a d", d=D),
                                in1=rstd[:, :].rearrange("p (t a) -> p t a", a=4)[:, :, :, None].to_broadcast([P, TPB, 4, D]),
                                op=ALU.mult).then_inc(s_sc, 1)
                        if step.extra == PROJECT_OUT and q == 3:
                            project_out(b)
                        if step.extra == ROUTE:
                            if q == 0:
                                dve.wait_ge(s_x2, b + 2)
                                settle(dve, s_mark)
                                ln_stats(b + B, b, 0)
                            if q == 1:
                                ln_apply(b + B, b, 0)
                            if q == 3:
                                add_router_bias(b)
                project_out(B - 1)
                dve.wait_ge(s_x2, B + 1)
                ln_stats(2 * B - 1, B - 1, 0)
                ln_apply(2 * B - 1, B - 1, 0)
                add_router_bias(B - 1)

            @block.scalar
            def _(act):
                a = nc.scalar

                def normed_out(bb, par):
                    act.wait_ge(s_lnT, bb + 1)
                    if not isinstance(bb, int):
                        settle(act, s_mark)
                    a.activation(tiles_of(xnT_all, bb), bank_t[:, par, :].rearrange("p (t k) -> p t k", k=P),
                                 ACT.Copy).then_inc(s_xnT, 1)

                for par in range(2):
                    normed_out(par, par)
                with act.Fori(1, B // 2) as k:
                    for par in range(2):
                        normed_out(k * 2 + par, par)

                def attention_projected(b):
                    act.wait_ge(s_y, b + 1)
                    a.activation(yT[:, :], bank_o[:, :], ACT.Copy).then_inc(s_yT, 1)

                def normed_x2(b):
                    act.wait_ge(s_lnT, b + (B + 1))
                    a.activation(xn2T[:, :, :], bank_m[:, :].rearrange("p (t k) -> p t k", k=P), ACT.Copy).then_inc(s_xn2T, 1)
                    a.activation(tiles_of(xn2, b), lnx[:, 0, :, :], ACT.Copy).then_inc(s_xn2, 1)

                for step in attention_steps(act):
                    n, par, b = step.number, step.parity, step.batch
                    up = (par + 1) % 2

                    def exp_tile(q):
                        if has_unit(step, 0):
                            wait(act, s_negm, n * 4 + (q + 1))
                            for h in range(2):
                                last = a.activation(prob_tile(h, q), bank_s[:, q % 2, h, 0:(q + 1) * P], ACT.Exp,
                                                    bias=negm[:, q, h:h + 1], accum_out=psums[:, q, h:h + 1])
                            last.then_inc(s_exp, 1)

                    def projected(i):
                        if has_unit(step, 2):
                            if i == 0:
                                wait(act, s_v[par], n * 8 + (16 - 8 * par))
                                wait(act, s_sc, n + 1)
                            wait(act, s_proj, n * 4 + (i + 9))
                            a.activation(raw[:, par, i, :], bank_m[:, 0:QKV], ACT.Copy).then_inc(s_raw, 1)

                    def qk_out(w):
                        if has_unit(step, 1):
                            wait(act, s_qkTp, n * 2 + (3 + w))
                            a.activation(qkT[:, up, w, :], bank_m[:, :], ACT.Copy).then_inc(s_qkT, 1)

                    projected(0)
                    exp_tile(0)
                    projected(1)

                    projected(2)
                    exp_tile(1)
                    if has_tile(step, 1, LAG):
                        wait(act, s_pt, n * 4)
                        a.activation(probT[:, :, :, 3 * P:T], bank_t[:, :, :].rearrange("p h (j k) -> p h j k", k=P),
                                     ACT.Copy).then_inc(s_probA, 1)
                    projected(3)

                    if step.extra == PROJECT_OUT:
                        attention_projected(b)
                    if has_unit(step, 2):
                        wait(act, s_ss, n + 2)
                        wait(act, s_raw, n * 4 + 12)
                        a.activation(sq[:, :, :], raw[:, par, :, 0:2 * P], ACT.Square, scale=D ** -0.5).then_inc(s_sq, 1)
                    exp_tile(2)
                    if step.extra == ROUTE:
                        normed_x2(b)

                    if has_unit(step, -1):
                        wait(act, s_pv, n + 1)
                        settle(act, s_mark)
                        p = step.pair_before
                        dst = outT[:, p, :] if isinstance(p, int) else \
                            outT[:, bass.ds(p, 1), :].rearrange("p a k -> p (a k)")
                        a.activation(dst, bank_o[:, :], ACT.Copy).then_inc(s_outT, 1)
                    qk_out(0)
                    qk_out(1)
                    exp_tile(3)
                attention_projected(B - 1)
                normed_x2(B - 1)

            @block.tensor
            def _(pe):
                t = nc.tensor
                pe.sem_inc(s_pv, 1)
                pe.wait_ge(s_const, 2)

                def normed(bb, par):
                    pe.wait_ge(s_lnx, bb + 1)
                    if not isinstance(bb, int):
                        pe.wait_ge(s_xnT, bb - 1)
                    for i in range(TPB):
                        last = t.transpose(bank_t[:, par, i * P:(i + 1) * P], lnx[:, par, i, :], ident[:, :])
                    last.then_inc(s_lnT, 1)

                for par in range(2):
                    normed(par, par)
                with pe.Fori(1, B // 2) as k:
                    for par in range(2):
                        normed(k * 2 + par, par)
                pe.wait_ge(s_load, 16 * LOADS)
                pe.wait_ge(s_xnT, B)

                def project_out(pairs):
                    for p in pairs:
                        last = t.matmul(bank_o[:, :], wo[:, p, :], outT[:, p, :], start=(p == 0), stop=(p == NP - 1),
                                        skip_group_check=True)
                    return last

                def projected_back(b, kt):
                    pe.wait_ge(s_qkT, kt)
                    pe.wait_ge(s_yT, b + 1)
                    for i in range(TPB):
                        last = t.transpose(bank_m[:, i * P:(i + 1) * P], yT[:, i * P:(i + 1) * P], ident[:, :])
                    last.then_inc(s_yt, 1)

                def normed_x2(b):
                    pe.wait_ge(s_lnx, b + (B + 1))
                    for i in range(TPB):
                        last = t.transpose(bank_m[:, i * P:(i + 1) * P], lnx[:, 0, i, :], ident[:, :])
                    last.then_inc(s_lnT, 1)

                def router(b):
                    pe.wait_ge(s_xn2T, b + 1)
                    for i in range(TPB):
                        last = t.matmul(bank_m[:, i * E:(i + 1) * E], xn2T[:, i, :], rw[:, :], start=True, stop=True)
                    last.then_inc(s_router, 1)

                for step in attention_steps(pe):
                    n, par, b = step.number, step.parity, step.batch
                    up = (par + 1) % 2

                    def scores(q):
                        if not has_unit(step, 0):
                            return
                        if q == 0:
                            wait(pe, s_qkT, n * 2 + 2)
                        wait(pe, s_exp, n * 4 + (q - 1))
                        keys = (q + 1) * P
                        for h in range(2):
                            t.matmul(bank_s[:, q % 2, h, 0:keys], qkT[D * h:D * h + D, par, 0, q * P:keys],
                                     qkT[D * h:D * h + D, par, 1, 0:keys], start=True, stop=False, skip_group_check=True)
                        for h in range(2):
                            last = t.matmul(bank_s[:, q % 2, h, q * P:keys], identb[:, :], causal[:, :],
                                            start=False, stop=True, skip_group_check=True)
                        last.then_inc(s_scores, 1)

                    def project(i):
                        if not has_unit(step, 2):
                            return
                        if i == 0:
                            wait(pe, s_w[par], n * 16 + (64 - 16 * par))
                            if step.extra == ROUTE:
                                wait(pe, s_x2, b + 2)
                            else:
                                wait(pe, s_logits, b + 1)
                                wait(pe, s_qkT, n * 2 + 2)
                                if isinstance(n, int) and n < 0:
                                    wait(pe, s_raw, 4 * (n + 2))
                        else:
                            wait(pe, s_raw, n * 4 + (8 + i))
                        t.matmul(bank_m[:, 0:QKV], xbuf[:, par, i * P:(i + 1) * P], wbuf[:, par, :],
                                 start=True, stop=True).then_inc(s_proj, 1)

                    def transposed(q):
                        if not has_tile(step, q, LAG):
                            return
                        r = (q - LAG) % 4
                        u = n + (q - LAG - r) // 4
                        wait(pe, s_norm, n * 4 + (q - LAG + 1))
                        if r == 0:
                            wait(pe, s_probA, u)
                        else:
                            wait(pe, s_probT, u * 3 + r)
                        for h in range(2):
                            for j in range(r + 1):
                                last = t.transpose(bank_t[:, h, j * P:(j + 1) * P],
                                                   prob[:, h, PROB_OFF[r] + j * P:PROB_OFF[r] + (j + 1) * P], ident[:, :])
                        last.then_inc(s_pt, 1)

                    def values():
                        if not has_unit(step, -1):
                            return
                        wait(pe, s_probT, n * 3)
                        wait(pe, s_probA, n)
                        wait(pe, s_v[up], n * 8 + (8 - 8 * up))
                        if step.extra == PROJECT_OUT:
                            wait(pe, s_yT, b + 1)
                        for j in range(TPB):
                            for h in range(2):
                                last = t.matmul(bank_o[D * h:D * h + D, j * P:T], vbuf[:, up, j, D * h:D * h + D],
                                                probT[:, h, j, j * P:T], start=(j == 0), stop=(j == TPB - 1),
                                                skip_group_check=True)
                        last.then_inc(s_pv, 1)

                    def qk_transposed(w):
                        if not has_unit(step, 1):
                            return
                        if w:
                            wait(pe, s_qkT, n * 2 + 3)
                        else:
                            wait(pe, s_rope, n + 2)
                            if step.extra == ROUTE:
                                wait(pe, s_xn2T, b + 1)
                            elif has_unit(step, 2):
                                wait(pe, s_raw, n * 4 + 12)
                            else:
                                wait(pe, s_qkT, n * 2 + 2)
                        for i in range(TPB):
                            last = t.transpose(bank_m[:, i * P:(i + 1) * P], rot[:, i, w * P:(w + 1) * P], ident[:, :])
                        last.then_inc(s_qkTp, 1)

                    scores(0)
                    project(0)
                    transposed(0)
                    if step.extra == PROJECT_OUT:
                        pe.wait_ge(s_outT, b * 8 + 8)
                        project_out(range(NP // 2))
                    project(1)

                    scores(1)
                    project(2)
                    transposed(1)
                    if step.extra == PROJECT_OUT:
                        project_out(range(NP // 2, NP)).then_inc(s_y, 1)
                    project(3)

                    scores(2)
                    if step.extra == ROUTE:
                        wait(pe, s_raw, n * 4 + 12)
                        normed_x2(b)
                    values()
                    transposed(2)
                    qk_transposed(0)

                    scores(3)
                    qk_transposed(1)
                    transposed(3)
                    if step.extra == PROJECT_OUT:
                        projected_back(b, n * 2 + 4)
                    if step.extra == ROUTE:
                        pe.wait_ge(s_qkT, n * 2 + 4)
                        router(b)
                pe.wait_ge(s_outT, UNITS)
                project_out(range(NP)).then_inc(s_y, 1)
                projected_back(B - 1, 2 * UNITS)
                pe.wait_ge(s_x2, B + 1)
                normed_x2(B - 1)
                router(B - 1)

        inner.close()
        experts(nc, x, xn2, logits, ident, before, onesb, s_mark, s_fill, 16 * (SLOTS // zero_rows), out_tiles,
                packed, expert_out, w1_in, b1_in, w2_in, b2_in)


def experts(nc, x, xn2, logits, ident, before, onesb, s_mark, s_fill, fill_count, out_tiles, packed, expert_out,
            w1_in, b1_in, w2_in, b2_in):
    w2_view = w2_in.rearrange("e (c p) n -> p e c n", p=P)
    packed_view = packed.rearrange("(e j p) c -> p e j c", e=E, p=P)
    expert_view = expert_out.rearrange("(e j p) c -> p e j c", e=E, p=P)

    with ExitStack() as ctx:
        def sb(name, shape, dt=F32):
            return ctx.enter_context(nc.sbuf_tensor(name, shape, dt))

        def psum(name, shape, dt=F32):
            return ctx.enter_context(nc.psum_tensor(name, shape, dt))

        def sem(name):
            return ctx.enter_context(nc.semaphore(name))

        b1 = sb("b1", [P, E * FC])
        b2 = sb("b2", [P, E, C])
        iota = sb("iota", [P, NT, E])
        cand = sb("cand", [P, NT, E])
        is_max = sb("is_max", [P, NT, E])
        pick = [sb(f"pick{k}", [P, NT, E]) for k in range(TOPK)]
        either = sb("either", [P, NT, E], BF16)
        total = sb("total", [P, NT, E])
        run_a = sb("run_a", [P, NT, E])
        run_b = sb("run_b", [P, NT, E])
        pos = sb("pos", [P, NT, E])
        top = [sb(f"top{k}", [P, NT]) for k in range(TOPK)]
        first = [sb(f"first{k}", [P, NT]) for k in range(TOPK)]
        place = [sb(f"place{k}", [P, NT]) for k in range(TOPK)]
        kept = [sb(f"kept{k}", [P, NT]) for k in range(TOPK)]
        slot = [sb(f"slot{k}", [P, NT]) for k in range(TOPK)]
        gate = [sb(f"gate{k}", [P, NT]) for k in range(TOPK)]
        tmp = [sb(f"tmp{k}", [P, NT]) for k in range(TOPK)]
        scatter_at = [sb(f"scatter_at{k}", [P, NT], U32) for k in range(TOPK)]
        gather_at = [sb(f"gather_at{k}", [P, NT], U32) for k in range(TOPK)]
        gap = sb("gap", [P, NT])
        egap = sb("egap", [P, NT])
        denom = sb("denom", [P, NT])
        xe = sb("xe", [P, 2, SJ, C])
        w1 = sb("w1", [P, 2, F])
        w2 = sb("w2", [P, 2, FC, C])
        xeT = sb("xeT", [P, 2, CAP])
        hT = sb("hT", [P, 2, FC, CAP])
        ye = sb("ye", [P, 2, SJ, C])
        rows = [sb(f"rows{k}", [P, 2, TPB, C]) for k in range(TOPK)]
        res = sb("res", [P, 2, TPB, C])

        bank_x = psum("bank_x", [P, 2, 512])
        bank_h = psum("bank_h", [P, 2, 2, 512])
        bank_y = psum("bank_y", [P, 2, 512])

        s_load = sem("s_load2")
        s_iota = sem("s_iota")
        s_r = sem("s_r")
        s_either = sem("s_either")
        s_pos = sem("s_pos")
        s_gap = sem("s_gap")
        s_egap = sem("s_egap")
        s_at = sem("s_at")
        s_scat = sem("s_scat")
        s_xe = [sem("s_xe0"), sem("s_xe1")]
        s_w1 = [sem("s_w1_0"), sem("s_w1_1")]
        s_w2 = [sem("s_w2_0"), sem("s_w2_1")]
        s_xTp = sem("s_xTp")
        s_xT = sem("s_xT")
        s_hp = sem("s_hp")
        s_h = sem("s_h")
        s_yp = sem("s_yp")
        s_ye = sem("s_ye")
        s_store = [sem("s_store0"), sem("s_store1")]
        s_rows = [sem("s_rows0"), sem("s_rows1")]
        s_mid = sem("s_mid")
        s_res = sem("s_res")
        s_out = [sem("s_out0"), sem("s_out1")]

        with nc.Block() as block:

            @block.sync
            def _(sp):
                for dst, src in ((b1[:, :], b1_in),
                                 (b2[:, :, :].rearrange("p e c -> p (e c)"),
                                  b2_in.rearrange("(a e) c -> a (e c)", a=1).to_broadcast([P, E * C]))):
                    sp.dma_start(dst, src).then_inc(s_load, 16)

                def load_slots(e, par):
                    src = packed_view[:, e] if isinstance(e, int) else \
                        packed_view[:, bass.ds(e, 1)].rearrange("p e j c -> p (e j) c")
                    sp.dma_start(xe[:, par, :, :], src).then_inc(s_xe[par], 16)

                def load_w1(e, par):
                    src = w1_in[e] if isinstance(e, int) else w1_in[bass.ds(e, 1)].rearrange("e p f -> p (e f)")
                    sp.dma_start(w1[:, par, :], src).then_inc(s_w1[par], 16)

                def load_w2(e, par):
                    src = w2_view[:, e] if isinstance(e, int) else \
                        w2_view[:, bass.ds(e, 1)].rearrange("p e c n -> p (e c) n")
                    sp.dma_start(w2[:, par, :, :], src).then_inc(s_w2[par], 16)

                def store_expert(e, par):
                    sp.wait_ge(s_ye, e * 2 + 3)
                    settle(sp, s_mark)
                    dst = expert_view[:, e] if isinstance(e, int) else \
                        expert_view[:, bass.ds(e, 1)].rearrange("p e j c -> p (e j) c")
                    sp.dma_start(dst, ye[:, par, :, :]).then_inc(s_store[par], 16)

                for e in range(2):
                    load_w1(e, e)
                    load_w2(e, e)
                sp.wait_ge(s_scat, 16 * TOPK * NT)
                for e in range(2):
                    load_slots(e, e)
                with sp.Fori(0, E // 2 - 1) as k:
                    for par in range(2):
                        e = k * 2 + par
                        sp.wait_ge(s_xTp, e + 1)
                        settle(sp, s_mark)
                        load_slots(e + 2, par)
                        sp.wait_ge(s_hp, e * 8 + 8)
                        settle(sp, s_mark)
                        load_w1(e + 2, par)
                        store_expert(e, par)
                        load_w2(e + 2, par)
                for par in range(2):
                    store_expert(E - 2 + par, par)
                with sp.Fori(0, B // 2) as k:
                    for par in range(2):
                        sp.wait_ge(s_res, k * 2 + (par + 1))
                        settle(sp, s_mark)
                        sp.dma_start(out_tiles[:, bass.ds(k * 2 + par, 1)].rearrange("p b t c -> p (b t) c"),
                                     res[:, par, :, :]).then_inc(s_out[par], 16)
                for par in range(2):
                    sp.wait_ge(s_out[par], 16 * (B // 2))

            @block.gpsimd
            def _(pool):
                g = nc.gpsimd
                g.iota(iota[:, :, :], pattern=[[0, NT], [1, E]], base=-E, channel_multiplier=0,
                       allow_small_or_imprecise_dtypes=True).then_inc(s_iota, 1)
                pool.wait_ge(s_at, 1)
                pool.wait_ge(s_fill, fill_count)
                for i in range(NT):
                    for k in range(TOPK):
                        g.indirect_dma_start(out=packed, out_offset=bass.IndirectOffsetOnAxis(ap=scatter_at[k][:, i:i + 1], axis=0),
                                             in_=xn2[:, i, :], in_offset=None, bounds_check=SLOTS - 1,
                                             oob_is_err=False).then_inc(s_scat, 16)
                for par in range(2):
                    pool.wait_ge(s_store[par], 16 * (E // 2))
                for b in range(B):
                    if b >= 2:
                        pool.wait_ge(s_res, b - 1)
                    for i in range(TPB):
                        for k in range(TOPK):
                            at = gather_at[k][:, b * TPB + i:b * TPB + i + 1]
                            g.indirect_dma_start(out=rows[k][:, b % 2, i, :], out_offset=None, in_=expert_out,
                                                 in_offset=bass.IndirectOffsetOnAxis(ap=at, axis=0),
                                                 bounds_check=SLOTS - 1, oob_is_err=False).then_inc(s_rows[b % 2], 16)

            @block.vector
            def _(dve):
                v = nc.vector
                steps = [0]
                dve.sem_inc(s_ye, 1)

                def then(ins):
                    steps[0] += 1
                    ins.then_inc(s_r, 1)
                    dve.wait_ge(s_r, steps[0])

                dve.wait_ge(s_load, 32)
                dve.wait_ge(s_iota, 1)

                def over_experts(t):
                    return t[:, :, None].to_broadcast([P, NT, E])

                for k in range(TOPK):
                    then(v.tensor_reduce(out=top[k][:, :], in_=logits[:, :, :], axis=AX.X, op=ALU.max))
                    if k == 1:
                        v.tensor_tensor(out=gap[:, :], in0=top[1][:, :], in1=top[0][:, :], op=ALU.subtract).then_inc(s_gap, 1)
                    then(v.tensor_tensor(out=is_max[:, :, :], in0=logits[:, :, :], in1=over_experts(top[k]), op=ALU.is_equal))
                    then(v.tensor_tensor(out=cand[:, :, :], in0=is_max[:, :, :], in1=iota[:, :, :], op=ALU.mult))
                    then(v.tensor_reduce(out=first[k][:, :], in_=cand[:, :, :], axis=AX.X, op=ALU.min))
                    then(v.tensor_tensor(out=pick[k][:, :, :], in0=iota[:, :, :], in1=over_experts(first[k]), op=ALU.is_equal))
                    if k == 0:
                        then(v.scalar_tensor_tensor(out=logits[:, :, :], in0=pick[0][:, :, :], scalar=-3.0e38,
                                                    in1=logits[:, :, :], op0=ALU.mult, op1=ALU.add))
                v.tensor_tensor(out=either[:, :, :], in0=pick[0][:, :, :], in1=pick[1][:, :, :], op=ALU.add).then_inc(s_either, 1)

                dve.wait_ge(s_pos, 1)
                then(v.tensor_copy(total[:, :, :], bank_h[:, 0, 1, :].rearrange("p (t e) -> p t e", e=E)))
                then(v.tensor_copy(run_a[:, :, :], total[:, :, :]))
                src, dst, d = run_a, run_b, 1
                while d < NT:
                    then(v.tensor_tensor(out=dst[:, d:, :], in0=src[:, d:, :], in1=src[:, :NT - d, :], op=ALU.add))
                    then(v.tensor_copy(dst[:, :d, :], src[:, :d, :]))
                    src, dst, d = dst, src, 2 * d
                then(v.tensor_tensor(out=dst[:, :, :], in0=src[:, :, :], in1=total[:, :, :], op=ALU.subtract))
                then(v.tensor_tensor(out=pos[:, :, :], in0=dst[:, :, :],
                                     in1=bank_h[:, 0, 0, :].rearrange("p (t e) -> p t e", e=E), op=ALU.add))
                for k in range(TOPK):
                    then(v.tensor_tensor(out=cand[:, :, :], in0=pick[k][:, :, :], in1=pos[:, :, :], op=ALU.mult))
                    then(v.tensor_reduce(out=place[k][:, :], in_=cand[:, :, :], axis=AX.X, op=ALU.add))
                    then(v.tensor_scalar(slot[k][:, :], first[k][:, :], float(CAP), float(SLOTS), ALU.mult, ALU.add))
                    then(v.tensor_tensor(out=slot[k][:, :], in0=slot[k][:, :], in1=place[k][:, :], op=ALU.add))
                    then(v.tensor_scalar(kept[k][:, :], place[k][:, :], float(CAP), None, ALU.is_lt))
                    then(v.tensor_scalar(tmp[k][:, :], kept[k][:, :], float(-2 * SLOTS), float(2 * SLOTS), ALU.mult, ALU.add))
                    then(v.tensor_tensor(out=scatter_at[k][:, :], in0=slot[k][:, :], in1=tmp[k][:, :], op=ALU.add))
                    then(v.tensor_scalar(gather_at[k][:, :], slot[k][:, :], float(SLOTS - 1), None, ALU.min))
                v.tensor_copy(tmp[0][:, :], kept[0][:, :]).then_inc(s_at, 1)

                dve.wait_ge(s_egap, 1)
                dve.wait_ge(s_at, 1)
                then(v.tensor_scalar(denom[:, :], egap[:, :], 1.0, None, ALU.add))
                then(v.reciprocal(gate[0][:, :], denom[:, :]))
                then(v.tensor_tensor(out=gate[1][:, :], in0=gate[0][:, :], in1=egap[:, :], op=ALU.mult))
                for k in range(TOPK):
                    then(v.tensor_tensor(out=tmp[k][:, :], in0=gate[k][:, :], in1=kept[k][:, :], op=ALU.mult))
                then(v.tensor_tensor(out=denom[:, :], in0=tmp[0][:, :], in1=tmp[1][:, :], op=ALU.add))
                then(v.tensor_scalar(denom[:, :], denom[:, :], 1e-9, None, ALU.add))
                then(v.reciprocal(gap[:, :], denom[:, :]))
                for k in range(TOPK):
                    then(v.tensor_tensor(out=gate[k][:, :], in0=tmp[k][:, :], in1=gap[:, :], op=ALU.mult))

                def add_bias(e, par):
                    bias = b2[:, e, :] if isinstance(e, int) else b2[:, bass.ds(e, 1), :].rearrange("p a c -> p (a c)")
                    wait(dve, s_store[par], e * 8 - 8 * par)
                    for part, (lo, n) in enumerate(((0, 4), (4, 1))):
                        dve.wait_ge(s_yp, e * 2 + (part + 1))
                        v.tensor_tensor(out=ye[:, par, lo:lo + n, :],
                                        in0=bank_y[:, part, 0:n * C].rearrange("p (j c) -> p j c", c=C),
                                        in1=bias[:, None, :].to_broadcast([P, n, C]), op=ALU.add).then_inc(s_ye, 1)

                def slots_out(e, par):
                    dve.wait_ge(s_xTp, e + 1)
                    v.tensor_copy(xeT[:, par, 0:512], bank_x[:, 0, :])
                    v.tensor_copy(xeT[:, par, 512:CAP], bank_x[:, 1, 0:CAP - 512]).then_inc(s_xT, 1)

                slots_out(0, 0)
                slots_out(1, 1)
                for par in range(2):
                    slots_out(2 + par, par)
                    add_bias(par, par)
                with dve.Fori(1, E // 2 - 1) as k:
                    for par in range(2):
                        slots_out(k * 2 + (2 + par), par)
                        add_bias(k * 2 + par, par)
                for par in range(2):
                    add_bias(E - 2 + par, par)

                def combine(k, par):
                    dve.wait_ge(s_rows[par], k * (16 * TPB * TOPK) + 16 * TPB * TOPK)
                    wait(dve, s_out[par], k * 16)

                    def column(t, i):
                        n = k * (2 * TPB) + (par * TPB + i)
                        return t[:, n:n + 1] if isinstance(n, int) else t[:, bass.ds(n, 1)]

                    for i in range(TPB):
                        last = v.scalar_tensor_tensor(
                            out=res[:, par, i, :], in0=rows[0][:, par, i, :], scalar=column(gate[0], i),
                            in1=column(x, i).rearrange("p a c -> p (a c)"), op0=ALU.mult, op1=ALU.add)
                    last.then_inc(s_mid, 1)
                    dve.wait_ge(s_mid, k * 2 + (par + 1))
                    for i in range(TPB):
                        last = v.scalar_tensor_tensor(
                            out=res[:, par, i, :], in0=rows[1][:, par, i, :], scalar=column(gate[1], i),
                            in1=res[:, par, i, :], op0=ALU.mult, op1=ALU.add)
                    last.then_inc(s_res, 1)

                for par in range(2):
                    combine(0, par)
                with dve.Fori(1, B // 2) as k:
                    for par in range(2):
                        combine(k, par)

            @block.scalar
            def _(act):
                a = nc.scalar
                act.wait_ge(s_gap, 1)
                a.activation(egap[:, :], gap[:, :], ACT.Exp).then_inc(s_egap, 1)
                act.wait_ge(s_load, 32)
                with act.Fori(0, E // 2) as k:
                    for par in range(2):
                        e = k * 2 + par
                        for c in range(FC):
                            for hf in range(2):
                                act.wait_ge(s_hp, e * 8 + (2 * c + hf + 1))
                                settle(act, s_mark)
                                a.activation(hT[:, par, c, hf * HALF:(hf + 1) * HALF], bank_h[:, c % 2, hf, 0:HALF],
                                             ACT.Gelu, bias=b1[:, bass.ds(e * FC + c, 1)]).then_inc(s_h, 1)

            @block.tensor
            def _(pe):
                t = nc.tensor
                pe.wait_ge(s_load, 32)
                pe.wait_ge(s_either, 1)
                t.matmul(bank_h[:, 0, 0, :], before[:, :], either[:, :, :].rearrange("p t e -> p (t e)"), start=True, stop=True)
                t.matmul(bank_h[:, 0, 1, :], onesb[:, :], either[:, :, :].rearrange("p t e -> p (t e)"),
                         start=True, stop=True).then_inc(s_pos, 1)

                def slots_in(e, par):
                    pe.wait_ge(s_xe[par], e * 8 + (16 - 8 * par))
                    wait(pe, s_xT, e)
                    for j in range(SJ):
                        last = t.transpose(bank_x[:, j // 4, (j % 4) * P:(j % 4 + 1) * P], xe[:, par, j, :], ident[:, :])
                    last.then_inc(s_xTp, 1)

                def hidden(e, par):
                    pe.wait_ge(s_xT, e + 1)
                    pe.wait_ge(s_w1[par], e * 8 + (16 - 8 * par))
                    for c in range(FC):
                        for hf in range(2):
                            wait(pe, s_h, e * 8 + (2 * c + hf - 3))
                            t.matmul(bank_h[:, c % 2, hf, 0:HALF], w1[:, par, c * P:(c + 1) * P],
                                     xeT[:, par, hf * HALF:(hf + 1) * HALF], start=True, stop=True).then_inc(s_hp, 1)

                def outputs(e, par):
                    pe.wait_ge(s_h, e * 8 + 8)
                    pe.wait_ge(s_w2[par], e * 8 + (16 - 8 * par))
                    wait(pe, s_ye, e * 2 + 1)
                    for j in range(SJ):
                        for c in range(FC):
                            last = t.matmul(bank_y[:, j // 4, (j % 4) * C:(j % 4 + 1) * C], hT[:, par, c, j * P:(j + 1) * P],
                                            w2[:, par, c, :], start=(c == 0), stop=(c == FC - 1))
                        if j >= 3:
                            last.then_inc(s_yp, 1)

                slots_in(0, 0)
                hidden(0, 0)
                slots_in(1, 1)
                with pe.Fori(0, E // 2 - 1) as k:
                    for e, par in ((k * 2 + 1, 1), (k * 2 + 2, 0)):
                        hidden(e, par)
                        slots_in(e + 1, 1 - par)
                        outputs(e - 1, 1 - par)
                hidden(E - 1, 1)
                outputs(E - 2, 0)
                outputs(E - 1, 1)


def rope_tables():
    import numpy as np
    inv_freq = np.float32(1.0) / np.float32(10000.0) ** (np.arange(0, D, 2, dtype=np.float32) / np.float32(D))
    angle = np.arange(T, dtype=np.float32)[:, None] * inv_freq
    cos, sin = np.cos(angle), np.sin(angle)

    def tiles(a):
        return np.ascontiguousarray(a.reshape(TPB, P, D).transpose(1, 0, 2)).astype(np.float32)

    return tiles(np.concatenate([cos, cos], axis=1)), tiles(np.concatenate([-sin, sin], axis=1))


def kernel(L0_attn_x, L0_attn_wqkv, L0_attn_wo, L0_attn_q_norm_w, L0_attn_k_norm_w, L0_ffn_router_w,
           L0_ffn_router_b, L0_ffn_w1, L0_ffn_b1, L0_ffn_w2, L0_ffn_b2):
    import numpy as np
    import concourse.bacc as bacc
    from concourse.bass_utils import run_bass_kernel_spmd

    cos, sin = rope_tables()
    laid = {
        "x": np.ascontiguousarray(L0_attn_x),
        "wqkv": np.ascontiguousarray(np.asarray(L0_attn_wqkv).reshape(3, NP, P, C).transpose(3, 1, 0, 2).reshape(C, NP, QKV)),
        "wo": np.ascontiguousarray(np.asarray(L0_attn_wo).reshape(C, NP, P).transpose(2, 1, 0)),
        "q_norm_w": np.ascontiguousarray(L0_attn_q_norm_w),
        "k_norm_w": np.ascontiguousarray(L0_attn_k_norm_w),
        "router_w": np.ascontiguousarray(np.asarray(L0_ffn_router_w).T),
        "router_b": np.ascontiguousarray(L0_ffn_router_b),
        "w1": np.ascontiguousarray(L0_ffn_w1),
        "b1": np.ascontiguousarray(np.asarray(L0_ffn_b1).reshape(E * FC, P).T),
        "w2": np.ascontiguousarray(L0_ffn_w2),
        "b2": np.ascontiguousarray(L0_ffn_b2),
        "cos": cos,
        "sin": sin,
    }
    nc = bacc.Bacc("TRN2", target_bir_lowering=False, num_devices=1)
    args = [nc.dram_tensor(f"in_{n}", a.shape, mybir.dt.from_np(a.dtype), kind="ExternalInput").ap() for n, a in laid.items()]
    out = nc.dram_tensor("out_0", (B, T, C), F32, kind="ExternalOutput").ap()
    build(nc, *args, out)
    r = run_bass_kernel_spmd(nc, [{f"in_{n}": a for n, a in laid.items()}], core_ids=[0])
    return r.results[0]["out_0"]
```

```python
import concourse.bass as bass
from concourse import mybir
from contextlib import ExitStack

F32 = mybir.dt.float32
F32R = mybir.dt.float32r
BF16 = mybir.dt.bfloat16
U32 = mybir.dt.uint32
ALU = mybir.AluOpType
ACT = mybir.ActivationFunctionType
AX = mybir.AxisListType

P = 128
B, T, C = 8, 512, 128
H, D = 16, 64
TPB = T // P
NT = B * TPB
NP = H // 2
RAW = 4
UNITS = B * NP
QKV = 3 * P
E, F, TOPK = 16, 512, 2
FC = F // P
CAP = -(-5 * B * T * TOPK // (4 * E))
SJ = CAP // P
HALF = CAP // 2
SLOTS = E * CAP
TOKENS = B * T
ROW = C + 1
NOWHERE = 2.0 ** 16
RMS_EPS, LN_EPS = 1e-6, 1e-5
MASKED = -1e30
LAG = 2
CHAIN = 15
PROB_OFF = [P * q * (q + 1) // 2 for q in range(TPB)]
PROB_COLS = P * TPB * (TPB + 1) // 2

PLAIN, NORM, PROJECT_OUT, NORM2, ROUTE, SCATTER = "plain", "norm", "project_out", "norm2", "route", "scatter"


class Step:

    def __init__(self, number, phase, extra=PLAIN, batch=0):
        self.number, self.phase, self.extra, self.batch = number, phase, extra, batch
        self.parity = phase % 2

    def pair(self, offset):
        return (self.phase + offset) % NP

    def slot(self, offset):
        return (self.phase + offset) % RAW


def attention_steps(eng):
    for s in range(-2, 5):
        yield Step(s, s % 8)
    with eng.Fori(0, B - 1) as b:
        for k, extra in enumerate((NORM, PLAIN, PLAIN, PLAIN, PROJECT_OUT, NORM2, ROUTE, SCATTER)):
            yield Step(b * 8 + (5 + k), (5 + k) % 8, extra, b + 1 if extra == NORM else b)
    for s in range(UNITS - 3, UNITS + 1):
        yield Step(s, s % 8)


def has_unit(step, offset):
    return not isinstance(step.number, int) or 0 <= step.number + offset < UNITS


def has_tile(step, q, lag):
    return not isinstance(step.number, int) or 0 <= 4 * step.number + q - lag < 4 * UNITS


def tiles_of(t, batch):
    if isinstance(batch, int):
        return t[:, batch * TPB:(batch + 1) * TPB]
    return t[:, bass.ds(batch * TPB, TPB)]


def tile(t, b, i):
    t = t[:, bass.ds(b * TPB + i, 1)]
    return t if len(t.shape) == 2 else t.rearrange("p a c -> p (a c)")


def settle(eng, s_mark):
    eng.sem_inc(s_mark, 1)


def wait(eng, sem, value):
    if isinstance(value, int) and value <= 0:
        return
    eng.wait_ge(sem, value)


def scatter_rows(nc, packed, xn2, scatter_at, s_scat):
    for i in range(TPB):
        for k in range(TOPK):
            nc.gpsimd.indirect_dma_start(
                out=packed, out_offset=bass.IndirectOffsetOnAxis(ap=scatter_at[:, k, i:i + 1], axis=0),
                in_=xn2[:, k, i, :], in_offset=None, bounds_check=SLOTS - 1, oob_is_err=False).then_inc(s_scat, 16)


def build(nc, x_in, wqkv_in, wo_in, qw_in, kw_in, rw_in, rb_in, w1_in, b1_in, w2_in, b2_in, cos_in, sin_in, out):
    packed = nc.dram_tensor("packed", (SLOTS, ROW), F32, kind="Internal").ap()
    results = nc.dram_tensor("results", (TOPK * TOKENS, C), F32, kind="Internal").ap()
    fill_rows = 8 * P
    fills = (SLOTS + TOPK * TOKENS) // fill_rows
    x_tiles = x_in.rearrange("b (t p) c -> p b t c", p=P)
    out_tiles = out.rearrange("b (t p) c -> p b t c", p=P)

    with ExitStack() as ctx:
        def sb(name, shape, dt=F32):
            return ctx.enter_context(nc.sbuf_tensor(name, shape, dt))

        def psum(name, shape, dt=F32):
            return inner.enter_context(nc.psum_tensor(name, shape, dt))

        def sem(name):
            return ctx.enter_context(nc.semaphore(name))

        inner = ctx.enter_context(ExitStack())

        def sba(name, shape, dt=F32):
            return inner.enter_context(nc.sbuf_tensor(name, shape, dt))

        x = sb("x", [P, NT, C])
        routed = sb("routed", [P, 6, NT])
        xn2 = sb("xn2", [P, TOPK, TPB, ROW])
        scatter_at = sb("scatter_at", [P, TOPK, TPB], U32)
        w1 = sb("w1", [P, 2, F])
        w2 = sb("w2", [P, 2, FC, C])
        b1 = sb("b1", [P, E * FC])
        b2 = sb("b2", [P, E, C])
        ident = sb("ident", [P, P])
        identb = sb("identb", [P, P], BF16)
        wqkv = sba("wqkv", [P, NP, QKV])
        w_hi = sba("w_hi", [P, NP, QKV], F32R)
        w_lo = sba("w_lo", [P, NP, QKV], F32R)
        wo = sba("wo", [P, NP, C])
        causal = sba("causal", [P, P], BF16)
        normw = sba("normw", [P, 2, D])
        cosw = sba("cosw", [P, TPB, 2, D])
        sinw = sba("sinw", [P, TPB, 2, D])
        cost = sba("cost", [P, TPB, D])
        sint = sba("sint", [P, TPB, D])
        xnT_hi = sba("xnT_hi", [P, T], F32R)
        xnT_lo = sba("xnT_lo", [P, T], F32R)
        raw = sba("raw", [P, RAW, TPB, QKV])
        sq = sba("sq", [P, TPB, 2 * P])
        ss = sba("ss", [P, TPB * 4])
        ssv = sba("ssv", [P, TPB * 4])
        rstd = sba("rstd", [P, TPB * 4])
        sc = sba("sc", [P, TPB, 2 * P])
        rot = sba("rot", [P, TPB, 2 * P])
        swp = sba("swp", [P, TPB, 2 * P])
        qkT = sba("qkT", [P, 2, 2, T])
        negm = sba("negm", [P, TPB, 2])
        psums = sba("psums", [P, 2, TPB, 2])
        rinv = sba("rinv", [P, TPB, 2])
        rinvw = sba("rinvw", [P, TPB, 2, D])
        prob = sba("prob", [P, 2, PROB_COLS])
        probT = sba("probT", [P, 2, TPB, T])
        invT = sba("invT", [P, T])
        outT = sba("outT", [P, NP, T])
        yT = sba("yT", [P, T])
        rw = sba("rw", [P, E])
        rb = sba("rb", [P, E])
        eps = sba("eps", [P, 2])
        empty = sba("empty", [P, fill_rows // P, ROW])
        xn2T = sba("xn2T", [P, TPB, P])
        before = sba("before", [P, P], BF16)
        onesb = sba("onesb", [P, P], BF16)
        half = sba("half", [P, 1])
        stats = sba("stats", [P, TPB, 6])
        mv = sba("mv", [P, TPB, 2])
        lnv = sba("lnv", [P, TPB])
        lnr = sba("lnr", [P, TPB])
        xn = sba("xn", [P, TPB, C])
        logits = sba("logits", [P, TPB, E])
        iota = sba("iota", [P, TPB, E])
        is_max = sba("is_max", [P, TPB, E])
        cand = sba("cand", [P, TPB, E])
        pick = sba("pick", [P, TOPK, TPB, E])
        either = sba("either", [P, TPB, E], BF16)
        pos = sba("pos", [P, TPB, E])
        taken = sba("taken", [P, E])
        place = sba("place", [P, TOPK, TPB, E])
        choice = sba("choice", [P, 6, TPB])
        slot = sba("slot", [P, TOPK, TPB])
        over = sba("over", [P, TOPK, TPB])

        bank_s = psum("bank_s", [P, 2, 2, 512])
        bank_t = psum("bank_t", [P, 2, 512])
        bank_o = psum("bank_o", [P, 512])
        bank_m = psum("bank_m", [P, 512])

        s_wqkv = sem("s_wqkv")
        s_load = sem("s_load")
        s_tables = sem("s_tables")
        s_x = sem("s_x")
        s_const = sem("s_const")
        s_mark = sem("s_mark")
        s_tab = sem("s_tab")
        s_bn = sem("s_bn")
        s_mv = sem("s_mv")
        s_lnv = sem("s_lnv")
        s_lnr = sem("s_lnr")
        s_lnx = sem("s_lnx")
        s_lnT = sem("s_lnT")
        s_xnT = sem("s_xnT")
        s_xlo = sem("s_xlo")
        s_whi = sem("s_whi")
        s_wlo = sem("s_wlo")
        s_proj = sem("s_proj")
        s_raw = sem("s_raw")
        s_probA = sem("s_probA")
        s_xn2T = sem("s_xn2T")
        s_router = sem("s_router")
        s_logits = sem("s_logits")
        s_sq = sem("s_sq")
        s_ss = sem("s_ss")
        s_ssv = sem("s_ssv")
        s_rstd = sem("s_rstd")
        s_sc = sem("s_sc")
        s_cos = sem("s_cos")
        s_sin = sem("s_sin")
        s_rope = sem("s_rope")
        s_qkTp = sem("s_qkTp")
        s_qkT = sem("s_qkT")
        s_scores = sem("s_scores")
        s_negm = sem("s_negm")
        s_exp = sem("s_exp")
        s_rinv = sem("s_rinv")
        s_rinvw = sem("s_rinvw")
        s_inv = sem("s_inv")
        s_invT = sem("s_invT")
        s_pt = sem("s_pt")
        s_probT = sem("s_probT")
        s_pv = sem("s_pv")
        s_outT = sem("s_outT")
        s_y = sem("s_y")
        s_yT = sem("s_yT")
        s_yt = sem("s_yt")
        s_x2 = sem("s_x2")
        s_r = sem("s_r")
        s_either = sem("s_either")
        s_counts = sem("s_counts")
        s_counted = sem("s_counted")
        s_at = sem("s_at")
        s_scat = sem("s_scat")
        s_routed = sem("s_routed")
        s_sent = sem("s_sent")
        s_empty = sem("s_empty")
        s_fill = sem("s_fill")
        s_goal = sem("s_goal")
        s_w1 = [sem("s_w1_0"), sem("s_w1_1")]
        s_w2 = [sem("s_w2_0"), sem("s_w2_1")]
        s_b = sem("s_b")

        def qk_heads(t):
            return t[:, :, :].rearrange("p t (a d) -> p t a d", d=D)

        def by_head(t):
            return t[:, :, :].rearrange("p t (a h d) -> p (t a) h d", a=2, h=2)

        def table(t):
            return t[:, :, :, :].rearrange("p t a d -> p (t a) d")

        def prob_tile(h, q):
            return prob[:, h, PROB_OFF[q]:PROB_OFF[q] + (q + 1) * P]

        with nc.Block() as block:

            @block.sync
            def _(sp):
                sp.dma_start(x[:, 0:TPB, :], x_tiles[:, 0, :, :]).then_inc(s_x, 16)
                sp.dma_start(wqkv[:, :, :], wqkv_in).then_inc(s_wqkv, 16)
                for dst, src in ((normw[:, 0, :], qw_in.rearrange("(a d) -> a d", a=1).to_broadcast([P, D])),
                                 (normw[:, 1, :], kw_in.rearrange("(a d) -> a d", a=1).to_broadcast([P, D])),
                                 (cost[:, :, :], cos_in), (sint[:, :, :], sin_in)):
                    sp.dma_start(dst, src).then_inc(s_tables, 16)
                for dst, src in ((wo[:, :, :], wo_in), (rw[:, :], rw_in),
                                 (rb[:, :], rb_in.rearrange("(a n) -> a n", a=1).to_broadcast([P, E]))):
                    sp.dma_start(dst, src).then_inc(s_load, 16)
                with sp.Fori(1, B) as b:
                    sp.wait_ge(s_x, b * 16)
                    settle(sp, s_mark)
                    sp.dma_start(x[:, bass.ds(b * TPB, TPB), :],
                                 x_tiles[:, bass.ds(b, 1), :, :].rearrange("p b t c -> p (b t) c")).then_inc(s_x, 16)
                sp.wait_ge(s_empty, 2)
                for i in range(SLOTS // fill_rows):
                    sp.dma_start(packed[i * fill_rows:(i + 1) * fill_rows, :].rearrange("(p r) c -> p r c", p=P),
                                 empty[:, :, :]).then_inc(s_fill, 16)
                for i in range(TOPK * TOKENS // fill_rows):
                    sp.dma_start(results[i * fill_rows:(i + 1) * fill_rows, :].rearrange("(p r) c -> p r c", p=P),
                                 empty[:, :, 0:C]).then_inc(s_fill, 16)
                for dst, src in ((b1[:, :], b1_in),
                                 (b2[:, :, :].rearrange("p e c -> p (e c)"),
                                  b2_in.rearrange("(a e) c -> a (e c)", a=1).to_broadcast([P, E * C]))):
                    sp.dma_start(dst, src).then_inc(s_b, 16)
                for e in range(2):
                    sp.dma_start(w1[:, e, :], w1_in[e]).then_inc(s_w1[e], 16)
                    sp.dma_start(w2[:, e, :, :], w2_in[e].rearrange("(c p) n -> p c n", p=P)).then_inc(s_w2[e], 16)

            @block.gpsimd
            def _(pool):
                g = nc.gpsimd
                g.memset(ident[:, :], 0.0)
                g.memset(identb[:, :], 0.0)
                g.memset(causal[:, :], 0.0)
                g.memset(half[:, :], -0.5)
                g.memset(eps[:, 0:1], RMS_EPS)
                g.memset(eps[:, 1:2], LN_EPS)
                g.memset(before[:, :], 1.0)
                g.memset(taken[:, :], 0.0)
                g.memset(onesb[:, :], 1.0).then_inc(s_const, 1)
                pool.wait_ge(s_const, 1)
                for m in (ident, identb):
                    g.affine_select(out=m[:, :], in_=m[:, :], compare_op=ALU.not_equal, fill=1.0, base=0,
                                    pattern=[[-1, P]], channel_multiplier=1)
                g.affine_select(out=causal[:, :], in_=causal[:, :], compare_op=ALU.is_ge, fill=MASKED, base=0,
                                pattern=[[-1, P]], channel_multiplier=1)
                g.affine_select(out=before[:, :], in_=before[:, :], compare_op=ALU.is_gt, fill=0.0, base=0,
                                pattern=[[1, P]], channel_multiplier=-1).then_inc(s_const, 1)
                pool.wait_ge(s_const, 2)

                def ln_rstd(count):
                    pool.wait_ge(s_mv, count + 1)
                    g.tensor_tensor(out=lnv[:, :], in0=mv[:, :, 1], in1=eps[:, 1:2].to_broadcast([P, TPB]),
                                    op=ALU.add).then_inc(s_lnv, 1)
                    pool.wait_ge(s_lnv, count + 1)
                    g.tensor_tensor(out=lnr[:, :], in0=lnv[:, :], in1=half[:, 0:1].to_broadcast([P, TPB]),
                                    op=ALU.pow).then_inc(s_lnr, 1)

                ln_rstd(0)
                g.memset(empty[:, :, 0:C], 0.0).then_inc(s_empty, 1)
                g.memset(empty[:, :, C:ROW], NOWHERE).then_inc(s_empty, 1)
                g.iota(xn2[:, :, :, C:ROW], pattern=[[TOKENS, TOPK], [P, TPB], [0, 1]], base=-T, channel_multiplier=1,
                       allow_small_or_imprecise_dtypes=True)
                g.iota(iota[:, :, :], pattern=[[0, TPB], [1, E]], base=-E, channel_multiplier=0,
                       allow_small_or_imprecise_dtypes=True).then_inc(s_const, 1)
                pool.sem_inc(s_sent, 1)

                for step in attention_steps(pool):
                    n, b = step.number, step.batch
                    if step.extra == NORM:
                        ln_rstd(b * 2 - 1)
                    if step.extra == NORM2:
                        ln_rstd(b * 2 + 2)
                    if has_unit(step, 1) and step.extra != SCATTER:
                        wait(pool, s_sin, n + 2)
                        wait(pool, s_cos, n + 2)
                        g.tensor_tensor(out=rot[:, :, :], in0=rot[:, :, :], in1=swp[:, :, :], op=ALU.add).then_inc(s_rope, 1)
                    if step.extra == SCATTER:
                        pool.wait_ge(s_fill, 16 * fills)
                        pool.wait_ge(s_at, b + 1)
                        scatter_rows(nc, packed, xn2, scatter_at, s_scat)
                    if has_unit(step, 2):
                        wait(pool, s_ss, n + 3)
                        g.tensor_tensor(out=ssv[:, :], in0=ss[:, :], in1=eps[:, 0:1].to_broadcast([P, 16]),
                                        op=ALU.add).then_inc(s_ssv, 1)
                        wait(pool, s_ssv, n + 3)
                        g.tensor_tensor(out=rstd[:, :], in0=ssv[:, :], in1=half[:, 0:1].to_broadcast([P, 16]),
                                        op=ALU.pow).then_inc(s_rstd, 1)
                        wait(pool, s_sc, n + 3)
                        src, dst, tab = by_head(sc), by_head(swp), table(sinw)
                        for lo, hi in ((0, D // 2), (D // 2, 0)):
                            last = g.tensor_tensor(
                                out=dst[:, :, :, lo:lo + D // 2], in0=src[:, :, :, hi:hi + D // 2],
                                in1=tab[:, :, None, lo:lo + D // 2].to_broadcast([P, 8, 2, D // 2]), op=ALU.mult)
                        last.then_inc(s_sin, 1)
                    if step.extra == SCATTER:
                        pool.wait_ge(s_scat, b * (16 * TPB * TOPK) + 16 * TPB * TOPK)
                        pool.sem_inc(s_sent, 1)
                ln_rstd(2 * B - 1)

            @block.vector
            def _(dve):
                v = nc.vector
                chain = [0]

                def ln_stats(count, b):
                    for i in range(TPB):
                        last = v.bn_stats(stats[:, i, :], row(b, i))
                    last.then_inc(s_bn, 1)
                    dve.wait_ge(s_bn, count + 1)
                    settle(dve, s_mark)
                    for i in range(TPB):
                        last = v.bn_aggr(mv[:, i, :], stats[:, i, :])
                    last.then_inc(s_mv, 1)

                def ln_apply(count, b, to):
                    dve.wait_ge(s_lnr, count + 1)
                    for i in range(TPB):
                        last = v.tensor_scalar(to[:, i, 0:C], row(b, i), mv[:, i, 0:1], lnr[:, i:i + 1],
                                               ALU.subtract, ALU.mult)
                    last.then_inc(s_lnx, 1)

                def ln2_apply(b):
                    dve.wait_ge(s_sent, b + 1)
                    ln_apply(b * 2 + 2 if not isinstance(b, int) else 2 * B - 1, b, xn2[:, 0])

                def ln2_rest(b):
                    dve.wait_ge(s_lnx, 2 * B if isinstance(b, int) else b * 2 + 3)
                    v.tensor_copy(xn2[:, 1, :, 0:C], xn2[:, 0, :, 0:C])
                    v.tensor_scalar(xn2[:, :, :, C:ROW], xn2[:, :, :, C:ROW], float(T), None, ALU.add).then_inc(s_goal, 1)

                def row(b, i):
                    if isinstance(b, int):
                        return x[:, b * TPB + i, :]
                    return x[:, bass.ds(b * TPB + i, 1), :].rearrange("p a c -> p (a c)")

                dve.wait_ge(s_x, 16)
                ln_stats(0, 0)
                ln_apply(0, 0, xn)

                def split_weights(p):
                    dve.wait_ge(s_whi, p + 1)
                    v.tensor_tensor(out=w_lo[:, p, :], in0=wqkv[:, p, :], in1=w_hi[:, p, :],
                                    op=ALU.subtract).then_inc(s_wlo, 1)

                def split_normed(b):
                    dve.wait_ge(s_xnT, b + 1)
                    v.tensor_tensor(out=xnT_lo[:, :], in0=bank_m[:, :], in1=xnT_hi[:, :], op=ALU.subtract).then_inc(s_xlo, 1)

                for p in range(2):
                    split_weights(p)
                split_normed(0)

                dve.wait_ge(s_tables, 16 * 4)
                for a in range(2):
                    scale = D ** -0.5 if a == 0 else 1.0
                    v.scalar_tensor_tensor(out=cosw[:, :, a, :], in0=cost[:, :, :], scalar=scale,
                                           in1=normw[:, a, None, :].to_broadcast([P, TPB, D]), op0=ALU.mult, op1=ALU.mult)
                    for lo, hi in ((0, D // 2), (D // 2, 0)):
                        last = v.scalar_tensor_tensor(
                            out=sinw[:, :, a, lo:lo + D // 2], in0=sint[:, :, lo:lo + D // 2], scalar=scale,
                            in1=normw[:, a, None, hi:hi + D // 2].to_broadcast([P, TPB, D // 2]), op0=ALU.mult, op1=ALU.mult)
                last.then_inc(s_tab, 1)
                dve.wait_ge(s_tab, 1)

                def project_out(b):
                    dve.wait_ge(s_yt, b + 1)
                    v.tensor_tensor(out=tiles_of(x, b), in0=tiles_of(x, b),
                                    in1=bank_m[:, :].rearrange("p (t c) -> p t c", c=C), op=ALU.add).then_inc(s_x2, 1)

                def add_router_bias(b):
                    dve.wait_ge(s_load, 16 * 3)
                    dve.wait_ge(s_router, b + 1)
                    v.tensor_tensor(out=logits[:, :, :], in0=bank_m[:, 0:TPB * E].rearrange("p (t e) -> p t e", e=E),
                                    in1=rb[:, None, :].to_broadcast([P, TPB, E]), op=ALU.add).then_inc(s_logits, 1)

                def then(b, ins):
                    chain[0] += 1
                    ins.then_inc(s_r, 1)
                    dve.wait_ge(s_r, b * CHAIN + chain[0])

                def over_experts(t):
                    return t[:, :, None].to_broadcast([P, TPB, E])

                def choose(b, k):
                    if k == 0:
                        chain[0] = 0
                        dve.wait_ge(s_logits, b + 1)
                    then(b, v.tensor_reduce(out=choice[:, k, :], in_=logits[:, :, :], axis=AX.X, op=ALU.max))
                    then(b, v.tensor_tensor(out=is_max[:, :, :], in0=logits[:, :, :], in1=over_experts(choice[:, k, :]),
                                            op=ALU.is_equal))
                    then(b, v.tensor_tensor(out=cand[:, :, :], in0=is_max[:, :, :], in1=iota[:, :, :], op=ALU.mult))
                    then(b, v.tensor_reduce(out=choice[:, 2 + k, :], in_=cand[:, :, :], axis=AX.X, op=ALU.min))
                    then(b, v.tensor_tensor(out=pick[:, k, :, :], in0=iota[:, :, :], in1=over_experts(choice[:, 2 + k, :]),
                                            op=ALU.is_equal))
                    if k == 0:
                        then(b, v.scalar_tensor_tensor(out=logits[:, :, :], in0=pick[:, 0, :, :], scalar=-3.0e38,
                                                       in1=logits[:, :, :], op0=ALU.mult, op1=ALU.add))
                    else:
                        v.tensor_tensor(out=either[:, :, :], in0=pick[:, 0, :, :], in1=pick[:, 1, :, :],
                                        op=ALU.add).then_inc(s_either, 1)

                def count_places(b):
                    dve.wait_ge(s_counts, b + 1)
                    then(b, v.tensor_tensor(out=pos[:, :, :], in0=bank_m[:, 0:TPB * E].rearrange("p (t e) -> p t e", e=E),
                                            in1=taken[:, None, :].to_broadcast([P, TPB, E]), op=ALU.add))
                    v.tensor_tensor(out=taken[:, :], in0=bank_m[:, TPB * E:(TPB + 1) * E], in1=taken[:, :],
                                    op=ALU.add).then_inc(s_counted, 1)

                def place_tokens(b):
                    dve.wait_ge(s_counted, b + 1)
                    dve.wait_ge(s_goal, b + 1)
                    then(b, v.tensor_tensor(out=place[:, :, :, :], in0=pick[:, :, :, :],
                                            in1=pos[:, None, :, :].to_broadcast([P, TOPK, TPB, E]), op=ALU.mult))
                    then(b, v.tensor_reduce(out=choice[:, 4:6, :], in_=place[:, :, :, :], axis=AX.X, op=ALU.add))
                    v.scalar_tensor_tensor(out=slot[:, :, :], in0=choice[:, 2:4, :], scalar=float(CAP),
                                           in1=choice[:, 4:6, :], op0=ALU.mult, op1=ALU.add)
                    then(b, v.tensor_scalar(over[:, :, :], choice[:, 4:6, :], float(CAP), float(2 * SLOTS),
                                            ALU.is_ge, ALU.mult))
                    v.scalar_tensor_tensor(out=scatter_at[:, :, :], in0=slot[:, :, :], scalar=float(SLOTS),
                                           in1=over[:, :, :], op0=ALU.add, op1=ALU.add).then_inc(s_at, 1)
                    v.tensor_copy(routed[:, :, b * TPB:(b + 1) * TPB] if isinstance(b, int) else
                                  routed[:, :, bass.ds(b * TPB, TPB)], choice[:, :, :]).then_inc(s_routed, 1)
                    assert chain[0] == CHAIN

                for step in attention_steps(dve):
                    n, b = step.number, step.batch
                    for q in range(4):
                        if has_unit(step, 0):
                            wait(dve, s_scores, n * 4 + (q + 1))
                            v.tensor_reduce(out=negm[:, q, :], in_=bank_s[:, q % 2, :, 0:(q + 1) * P], axis=AX.X,
                                            op=ALU.max, negate=True).then_inc(s_negm, 1)
                        if q == 1 and has_unit(step, -1):
                            wait(dve, s_exp, n * 4)
                            v.reciprocal(rinv[:, :, :], psums[:, 1 - step.parity, :, :]).then_inc(s_rinv, 1)
                            wait(dve, s_rinv, n)
                            v.tensor_copy(rinvw[:, :, :, :], rinv[:, :, :, None].to_broadcast([P, TPB, 2, D])).then_inc(s_rinvw, 1)
                        if q == 0 and step.extra == NORM2:
                            dve.wait_ge(s_x2, b + 1)
                            settle(dve, s_mark)
                            ln_stats(b * 2 + 2, b)
                        if q == 0 and step.extra == NORM:
                            dve.wait_ge(s_x, b * 16 + 16)
                            settle(dve, s_mark)
                            ln_stats(b * 2 - 1, b)
                        if q == 0 and has_tile(step, q, LAG):
                            r = (q - LAG) % 4
                            wait(dve, s_pt, n * 4 + (q - LAG + 1))
                            v.tensor_copy(
                                probT[:, :, 0:r + 1, r * P:(r + 1) * P],
                                bank_t[:, :, 0:(r + 1) * P].rearrange("p h (j k) -> p h j k", k=P)).then_inc(s_probT, 1)
                        if q == 0 and has_unit(step, 1):
                            wait(dve, s_sc, n + 2)
                            wait(dve, s_qkTp, n * 2 + 2)
                            v.tensor_tensor(out=by_head(rot), in0=by_head(sc),
                                            in1=table(cosw)[:, :, None, :].to_broadcast([P, 8, 2, D]),
                                            op=ALU.mult).then_inc(s_cos, 1)
                        if q == 1 and step.extra == SCATTER:
                            dve.wait_ge(s_cos, n + 2)
                            dve.wait_ge(s_sin, n + 2)
                            v.tensor_tensor(out=rot[:, :, :], in0=rot[:, :, :], in1=swp[:, :, :], op=ALU.add).then_inc(s_rope, 1)
                        if q == 2 and step.extra == NORM:
                            split_normed(b)
                        if q == 0 and isinstance(n, int) and n + 4 < NP:
                            split_weights(n + 4)
                        if q == 2 and step.extra == PROJECT_OUT:
                            project_out(b)
                        if q == 2 and has_unit(step, 2):
                            wait(dve, s_sq, n + 3)
                            v.tensor_reduce(out=ss[:, :], in_=qk_heads(sq), axis=AX.X, op=ALU.add).then_inc(s_ss, 1)
                        if q == 3 and has_tile(step, q, LAG):
                            r = (q - LAG) % 4
                            wait(dve, s_pt, n * 4 + (q - LAG + 1))
                            v.tensor_copy(
                                probT[:, :, 0:r + 1, r * P:(r + 1) * P],
                                bank_t[:, :, 0:(r + 1) * P].rearrange("p h (j k) -> p h j k", k=P)).then_inc(s_probT, 1)
                        if q == 2 and step.extra == NORM2:
                            add_router_bias(b)
                        if q == 2 and step.extra == ROUTE:
                            count_places(b)
                        if q == 2 and has_unit(step, -1):
                            wait(dve, s_invT, n)
                            wait(dve, s_pv, n + 1)
                            v.tensor_tensor(out=outT[:, step.pair(-1), :], in0=bank_o[:, :], in1=invT[:, :], op=ALU.mult).then_inc(s_outT, 1)
                        if q == 3 and has_unit(step, 2):
                            wait(dve, s_rstd, n + 3)
                            wait(dve, s_sin, n + 2)
                            v.tensor_tensor(
                                out=qk_heads(sc), in0=raw[:, step.slot(2), :, 0:2 * P].rearrange("p t (a d) -> p t a d", d=D),
                                in1=rstd[:, :].rearrange("p (t a) -> p t a", a=4)[:, :, :, None].to_broadcast([P, TPB, 4, D]),
                                op=ALU.mult).then_inc(s_sc, 1)
                        if step.extra == NORM:
                            if q == 1:
                                ln_apply(b * 2 - 1, b, xn)
                        if step.extra == NORM2:
                            if q == 1:
                                ln2_apply(b)
                            if q == 2:
                                ln2_rest(b)
                        if step.extra == SCATTER and q == 0:
                            place_tokens(b)
                        if step.extra == ROUTE:
                            if q < 2:
                                choose(b, q)
                project_out(B - 1)
                dve.wait_ge(s_x2, B)
                ln_stats(2 * B - 1, B - 1)
                ln2_apply(B - 1)
                ln2_rest(B - 1)
                add_router_bias(B - 1)
                for k in range(TOPK):
                    choose(B - 1, k)
                count_places(B - 1)
                place_tokens(B - 1)

            @block.scalar
            def _(act):
                a = nc.scalar

                def normed_out(count):
                    act.wait_ge(s_lnT, count + 1)
                    a.activation(xnT_hi[:, :], bank_m[:, :], ACT.Copy).then_inc(s_xnT, 1)

                act.wait_ge(s_wqkv, 16)
                for p in range(2):
                    a.activation(w_hi[:, p, :], wqkv[:, p, :], ACT.Copy).then_inc(s_whi, 1)
                normed_out(0)
                for p in range(2, NP):
                    a.activation(w_hi[:, p, :], wqkv[:, p, :], ACT.Copy).then_inc(s_whi, 1)

                def attention_projected(b, bank):
                    act.wait_ge(s_y, b + 1)
                    a.activation(yT[:, :], bank, ACT.Copy).then_inc(s_yT, 1)

                def normed_x2(b):
                    act.wait_ge(s_lnT, 2 * B if isinstance(b, int) else b * 2 + 3)
                    a.activation(xn2T[:, :, :], bank_m[:, :].rearrange("p (t k) -> p t k", k=P), ACT.Copy).then_inc(s_xn2T, 1)

                for step in attention_steps(act):
                    n, par, b = step.number, step.parity, step.batch
                    up = (par + 1) % 2

                    def exp_head(q, h, par):
                        return a.activation(prob_tile(h, q), bank_s[:, q % 2, h, 0:(q + 1) * P], ACT.Exp,
                                            bias=negm[:, q, h:h + 1], accum_out=psums[:, par, q, h:h + 1])

                    def exp_tile(q):
                        if has_unit(step, 0):
                            wait(act, s_negm, n * 4 + (q + 1))
                            exp_head(q, 0, par)
                            if q < 3:
                                exp_head(q, 1, par).then_inc(s_exp, 1)

                    def exp_left():
                        if has_unit(step, -1):
                            exp_head(3, 1, up).then_inc(s_exp, 1)

                    def projected(i):
                        if has_unit(step, 2):
                            wait(act, s_proj, n * 4 + (i + 9))
                            a.activation(raw[:, step.slot(2), i, :], bank_m[:, 0:QKV], ACT.Copy).then_inc(s_raw, 1)

                    def qk_out(w):
                        if has_unit(step, 1):
                            wait(act, s_qkTp, n * 2 + (3 + w))
                            a.activation(qkT[:, up, :, w * (T // 2):(w + 1) * (T // 2)],
                                         bank_m[:, :].rearrange("p (a k) -> p a k", a=2), ACT.Copy).then_inc(s_qkT, 1)

                    projected(0)
                    exp_left()
                    exp_tile(0)
                    projected(1)

                    projected(2)
                    exp_tile(1)
                    if has_tile(step, 1, LAG):
                        wait(act, s_pt, n * 4)
                        a.activation(probT[:, :, :, 3 * P:T], bank_t[:, :, :].rearrange("p h (j k) -> p h j k", k=P),
                                     ACT.Copy).then_inc(s_probA, 1)
                    projected(3)

                    if step.extra == PROJECT_OUT:
                        attention_projected(b, bank_o[:, :])
                    if has_unit(step, 2):
                        wait(act, s_ss, n + 2)
                        wait(act, s_raw, n * 4 + 12)
                        a.activation(sq[:, :, :], raw[:, step.slot(2), :, 0:2 * P], ACT.Square, scale=D ** -0.5).then_inc(s_sq, 1)
                    if step.extra == NORM:
                        normed_out(b * 2 - 1)
                    if step.extra == NORM2:
                        normed_x2(b)
                    exp_tile(2)
                    if step.extra not in (NORM2, ROUTE):
                        qk_out(0)
                    if has_tile(step, 2, LAG):
                        wait(act, s_pt, n * 4 + 1)
                        if has_unit(step, -1):
                            wait(act, s_inv, n)
                        a.activation(probT[:, :, 0, 0:P], bank_t[:, :, 0:P], ACT.Copy).then_inc(s_probA, 1)
                    if has_unit(step, -1):
                        wait(act, s_inv, n)
                        a.activation(invT[:, :].rearrange("p (a k) -> p a k", a=2), bank_t[:, :, P:3 * P],
                                     ACT.Copy).then_inc(s_invT, 1)
                    if step.extra in (NORM2, ROUTE):
                        qk_out(0)
                    qk_out(1)
                    exp_tile(3)
                attention_projected(B - 1, bank_s[:, 0, 0, :])
                normed_x2(B - 1)

            @block.tensor
            def _(pe):
                t = nc.tensor
                pe.sem_inc(s_pv, 1)
                pe.wait_ge(s_const, 2)

                def normed(count, xn):
                    pe.wait_ge(s_lnx, count + 1)
                    for i in range(TPB):
                        last = t.transpose(bank_m[:, i * P:(i + 1) * P], xn[:, i, 0:C], ident[:, :])
                    last.then_inc(s_lnT, 1)

                normed(0, xn)

                def project_out(pairs, bank):
                    for p in pairs:
                        last = t.matmul(bank, wo[:, p, :], outT[:, p, :], start=(p == 0), stop=(p == NP - 1),
                                        skip_group_check=True)
                    return last

                def projected_back(b):
                    pe.wait_ge(s_yT, b + 1)
                    for i in range(TPB):
                        last = t.transpose(bank_m[:, i * P:(i + 1) * P], yT[:, i * P:(i + 1) * P], ident[:, :])
                    last.then_inc(s_yt, 1)

                def counts(b):
                    pe.wait_ge(s_either, b + 1)
                    for i in range(TPB):
                        for j in range(i + 1):
                            t.matmul(bank_m[:, i * E:(i + 1) * E], (before if j == i else onesb)[:, :], either[:, j, :],
                                     start=(j == 0), stop=(j == i), skip_group_check=True)
                    for j in range(TPB):
                        last = t.matmul(bank_m[:, TPB * E:(TPB + 1) * E], onesb[:, :], either[:, j, :],
                                        start=(j == 0), stop=(j == TPB - 1), skip_group_check=True)
                    last.then_inc(s_counts, 1)

                def router(b):
                    pe.wait_ge(s_xn2T, b + 1)
                    for i in range(TPB):
                        last = t.matmul(bank_m[:, i * E:(i + 1) * E], xn2T[:, i, :], rw[:, :], start=True, stop=True)
                    last.then_inc(s_router, 1)

                for step in attention_steps(pe):
                    n, par, b = step.number, step.parity, step.batch
                    up = (par + 1) % 2

                    def scores(q):
                        if not has_unit(step, 0):
                            return
                        if q in (0, 2):
                            wait(pe, s_qkT, n * 2 + (1 + q // 2))
                        wait(pe, s_exp, n * 4 + (q - 1))
                        keys = (q + 1) * P
                        for h in range(2):
                            t.matmul(bank_s[:, q % 2, h, 0:keys], qkT[D * h:D * h + D, par, 0, q * P:keys],
                                     qkT[D * h:D * h + D, par, 1, 0:keys], start=True, stop=False, skip_group_check=True)
                        for h in range(2):
                            last = t.matmul(bank_s[:, q % 2, h, q * P:keys], identb[:, :], causal[:, :],
                                            start=False, stop=True, skip_group_check=True)
                        last.then_inc(s_scores, 1)

                    def project(i):
                        if not has_unit(step, 2):
                            return
                        if i == 0:
                            if isinstance(n, int) and n < 0:
                                pe.wait_ge(s_wlo, n + 3 if n < 4 else NP)
                            if isinstance(n, int) and n < 0:
                                if n == -2:
                                    pe.wait_ge(s_xlo, 1)
                                wait(pe, s_raw, 4 * (n + 2))
                            wait(pe, s_qkT, n * 2 + 2)
                        else:
                            wait(pe, s_raw, n * 4 + (8 + i))
                        tokens, p = slice(i * P, (i + 1) * P), step.pair(2)
                        t.matmul(bank_m[:, 0:QKV], xnT_hi[:, tokens], w_hi[:, p, :], start=True, stop=False)
                        t.matmul(bank_m[:, 0:QKV], xnT_hi[:, tokens], w_lo[:, p, :], start=False, stop=False)
                        t.matmul(bank_m[:, 0:QKV], xnT_lo[:, tokens], w_hi[:, p, :],
                                 start=False, stop=True).then_inc(s_proj, 1)

                    def transposed(q):
                        if not has_tile(step, q, LAG):
                            return
                        r = (q - LAG) % 4
                        u = n + (q - LAG - r) // 4
                        if not has_unit(step, 0):
                            wait(pe, s_exp, n * 4 + (q - LAG + 1))
                        if r == 0:
                            wait(pe, s_probA, u * 2)
                        elif r > 1:
                            wait(pe, s_probT, u * 2 + (r - 1))
                        elif has_unit(step, -1):
                            wait(pe, s_invT, n)
                        else:
                            wait(pe, s_probA, u * 2 + 1)
                        for h in range(2):
                            for j in range(r + 1):
                                last = t.transpose(bank_t[:, h, j * P:(j + 1) * P],
                                                   prob[:, h, PROB_OFF[r] + j * P:PROB_OFF[r] + (j + 1) * P], ident[:, :])
                        last.then_inc(s_pt, 1)

                    def values():
                        if not has_unit(step, -1):
                            return
                        wait(pe, s_rinvw, n)
                        wait(pe, s_probA, n * 2)
                        wait(pe, s_probT, n * 2)
                        if step.extra == PROJECT_OUT:
                            wait(pe, s_yT, b + 1)
                        for j in range(TPB):
                            for h in range(2):
                                last = t.matmul(bank_o[D * h:D * h + D, j * P:T], raw[:, step.slot(-1), j, 2 * P + D * h:2 * P + D * h + D],
                                                probT[:, h, j, j * P:T], start=(j == 0), stop=(j == TPB - 1),
                                                skip_group_check=True)
                        last.then_inc(s_pv, 1)

                    def inverse_sums():
                        if not has_unit(step, -1):
                            return
                        for i in range(TPB):
                            last = t.transpose(bank_t[:, i // 2, (i % 2 + 1) * P:(i % 2 + 2) * P],
                                               rinvw[:, i, :, :].rearrange("p h d -> p (h d)"), ident[:, :])
                        last.then_inc(s_inv, 1)

                    def qk_transposed(w):
                        if not has_unit(step, 1):
                            return
                        if w:
                            wait(pe, s_qkT, n * 2 + 3)
                        else:
                            wait(pe, s_rope, n + 2)
                            if step.extra == NORM:
                                wait(pe, s_xlo, b + 1)
                            elif step.extra == PROJECT_OUT:
                                wait(pe, s_x2, b + 1)
                            elif step.extra == NORM2:
                                wait(pe, s_logits, b + 1)
                            elif step.extra == ROUTE:
                                wait(pe, s_counted, b + 1)
                            elif has_unit(step, 2):
                                wait(pe, s_raw, n * 4 + 12)
                            else:
                                wait(pe, s_qkT, n * 2 + 2)
                        for a in range(2):
                            for i in range(2):
                                last = t.transpose(bank_m[:, (2 * a + i) * P:(2 * a + i + 1) * P],
                                                   rot[:, 2 * w + i, a * P:(a + 1) * P], ident[:, :])
                        last.then_inc(s_qkTp, 1)

                    scores(0)
                    project(0)
                    transposed(0)
                    if step.extra == PROJECT_OUT:
                        pe.wait_ge(s_load, 16 * 3)
                        pe.wait_ge(s_outT, b * 8 + 8)
                        project_out(range(NP // 2), bank_o[:, :])
                    project(1)

                    scores(1)
                    project(2)
                    transposed(1)
                    if step.extra == PROJECT_OUT:
                        project_out(range(NP // 2, NP), bank_o[:, :]).then_inc(s_y, 1)
                    project(3)

                    if isinstance(n, int) and n == UNITS:
                        project_out(range(NP - 1), bank_s[:, 0, 0, :])
                    scores(2)
                    if step.extra in (NORM, PROJECT_OUT, NORM2):
                        wait(pe, s_raw, n * 4 + 12)
                        if step.extra == NORM:
                            normed(b * 2 - 1, xn)
                        if step.extra == PROJECT_OUT:
                            projected_back(b)
                        if step.extra == NORM2:
                            normed(b * 2 + 2, xn2[:, 0])
                    if step.extra in (PLAIN, SCATTER):
                        values()
                        qk_transposed(0)
                        transposed(2)
                        inverse_sums()
                        scores(3)
                        qk_transposed(1)
                    elif step.extra in (NORM2, ROUTE):
                        values()
                        if step.extra == NORM2:
                            router(b)
                        else:
                            pe.wait_ge(s_raw, n * 4 + 12)
                            counts(b)
                        transposed(2)
                        inverse_sums()
                        qk_transposed(0)
                        scores(3)
                        qk_transposed(1)
                    else:
                        values()
                        qk_transposed(0)
                        transposed(2)
                        inverse_sums()
                        scores(3)
                        qk_transposed(1)
                    transposed(3)
                pe.wait_ge(s_outT, UNITS)
                project_out([NP - 1], bank_s[:, 0, 0, :]).then_inc(s_y, 1)
                projected_back(B - 1)
                normed(2 * B - 1, xn2[:, 0])
                router(B - 1)
                pe.wait_ge(s_logits, B)
                counts(B - 1)

        inner.close()
        experts(nc, x, xn2, scatter_at, routed, w1, w2, b1, b2, ident, s_mark, s_at, s_scat, s_routed, s_w1, s_w2, s_b,
                out_tiles, packed, results, w1_in, w2_in)


def experts(nc, x, xn2, scatter_at, routed, w1, w2, b1, b2, ident, s_mark, s_at, s_scat, s_routed, s_w1, s_w2, s_b,
            out_tiles, packed, results, w1_in, w2_in):
    w2_view = w2_in.rearrange("e (c p) n -> p e c n", p=P)
    packed_view = packed.rearrange("(e j p) c -> p e j c", e=E, p=P)
    results_view = results.rearrange("(k b t p) c -> p k b t c", k=TOPK, b=B, p=P)

    with ExitStack() as ctx:
        def sb(name, shape, dt=F32):
            return ctx.enter_context(nc.sbuf_tensor(name, shape, dt))

        def psum(name, shape, dt=F32):
            return ctx.enter_context(nc.psum_tensor(name, shape, dt))

        def sem(name):
            return ctx.enter_context(nc.semaphore(name))

        kept = [sb(f"kept{k}", [P, NT]) for k in range(TOPK)]
        gate = [sb(f"gate{k}", [P, NT]) for k in range(TOPK)]
        tmp = [sb(f"tmp{k}", [P, NT]) for k in range(TOPK)]
        goals = sb("goals", [P, E, SJ], U32)
        goal = sb("goal", [P, 2, SJ], U32)
        gap = sb("gap", [P, NT])
        egap = sb("egap", [P, NT])
        denom = sb("denom", [P, NT])
        xe = sb("xe", [P, 2, SJ, ROW])
        w1_hi = sb("w1_hi", [P, 2, F], F32R)
        w1_lo = sb("w1_lo", [P, 2, F], F32R)
        xeT_hi = sb("xeT_hi", [P, 2, CAP], F32R)
        xeT_lo = sb("xeT_lo", [P, 2, CAP], F32R)
        hT = sb("hT", [P, 2, FC, CAP])
        ye = sb("ye", [P, 2, SJ, C])
        rows = [sb(f"rows{k}", [P, NT, C]) for k in range(TOPK)]

        bank_x = psum("bank_x", [P, 2, 512])
        bank_h = psum("bank_h", [P, 2, 2, 512])
        bank_y = psum("bank_y", [P, 2, 512])

        s_g = sem("s_g")
        s_gap = sem("s_gap")
        s_egap = sem("s_egap")
        s_goals = sem("s_goals")
        s_xe = [sem("s_xe0"), sem("s_xe1")]
        s_xTp = sem("s_xTp")
        s_xT = sem("s_xT")
        s_xhi = sem("s_xhi")
        s_w1hi = sem("s_w1hi")
        s_w1s = sem("s_w1s")
        s_hp = sem("s_hp")
        s_h = sem("s_h")
        s_yp = sem("s_yp")
        s_ye = sem("s_ye")
        s_store = [sem("s_store0"), sem("s_store1")]
        s_rows = [sem("s_rows0"), sem("s_rows1")]
        s_mid = sem("s_mid")
        s_gates = sem("s_gates")
        s_second = sem("s_second")
        s_res = sem("s_res")
        s_out = [sem("s_out0"), sem("s_out1")]

        with nc.Block() as block:

            @block.sync
            def _(sp):
                def load_slots(e, par):
                    src = packed_view[:, e] if isinstance(e, int) else \
                        packed_view[:, bass.ds(e, 1)].rearrange("p e j c -> p (e j) c")
                    sp.dma_start(xe[:, par, :, :], src).then_inc(s_xe[par], 16)

                def load_w1(e, par):
                    src = w1_in[e] if isinstance(e, int) else w1_in[bass.ds(e, 1)].rearrange("e p f -> p (e f)")
                    sp.dma_start(w1[:, par, :], src).then_inc(s_w1[par], 16)

                def load_w2(e, par):
                    src = w2_view[:, e] if isinstance(e, int) else \
                        w2_view[:, bass.ds(e, 1)].rearrange("p e c n -> p (e c) n")
                    sp.dma_start(w2[:, par, :, :], src).then_inc(s_w2[par], 16)

                sp.wait_ge(s_scat, 16 * TOPK * NT)
                for e in range(2):
                    load_slots(e, e)
                with sp.Fori(0, E // 2 - 1) as k:
                    for par in range(2):
                        e = k * 2 + par
                        sp.wait_ge(s_w1s, e + 1)
                        settle(sp, s_mark)
                        load_w1(e + 2, par)
                        sp.wait_ge(s_xT, e + 1)
                        settle(sp, s_mark)
                        load_slots(e + 2, par)
                        sp.wait_ge(s_ye, e * 2 + 3)
                        settle(sp, s_mark)
                        load_w2(e + 2, par)

                def load_rows(b, par):
                    for k in range(TOPK):
                        src = results_view[:, k, b] if isinstance(b, int) else \
                            results_view[:, k, bass.ds(b, 1)].rearrange("p b t c -> p (b t) c")
                        sp.dma_start(tiles_of(rows[k], b), src).then_inc(s_rows[par], 16)

                for par in range(2):
                    sp.wait_ge(s_store[par], 16 * SJ * (E // 2))
                for par in range(2):
                    load_rows(par, par)
                with sp.Fori(0, B // 2 - 1) as k:
                    for par in range(2):
                        sp.wait_ge(s_rows[par], k * (16 * TOPK) + 16 * TOPK)
                        settle(sp, s_mark)
                        load_rows(k * 2 + (par + 2), par)
                        sp.wait_ge(s_res, k * 2 + (par + 1))
                        settle(sp, s_mark)
                        sp.dma_start(out_tiles[:, bass.ds(k * 2 + par, 1)].rearrange("p b t c -> p (b t) c"),
                                     tiles_of(rows[0], k * 2 + par)).then_inc(s_out[par], 16)
                for par in range(2):
                    sp.wait_ge(s_res, B - 1 + par)
                    sp.dma_start(out_tiles[:, B - 2 + par], tiles_of(rows[0], B - 2 + par)).then_inc(s_out[par], 16)
                for par in range(2):
                    sp.wait_ge(s_out[par], 16 * (B // 2))

            @block.gpsimd
            def _(pool):
                g = nc.gpsimd

                pool.wait_ge(s_at, B)
                scatter_rows(nc, packed, xn2, scatter_at, s_scat)

                def scatter(e, par):
                    pool.wait_ge(s_ye, e * 2 + 3)
                    settle(pool, s_mark)
                    for j in range(SJ):
                        g.indirect_dma_start(out=results, out_offset=bass.IndirectOffsetOnAxis(ap=goal[:, par, j:j + 1], axis=0),
                                             in_=ye[:, par, j, :], in_offset=None, bounds_check=TOPK * TOKENS - 1,
                                             oob_is_err=False).then_inc(s_store[par], 16)

                with pool.Fori(0, E // 2) as k:
                    for par in range(2):
                        scatter(k * 2 + par, par)

            @block.vector
            def _(dve):
                v = nc.vector
                steps = [0]
                dve.sem_inc(s_ye, 1)

                def then(ins):
                    steps[0] += 1
                    ins.then_inc(s_g, 1)
                    dve.wait_ge(s_g, steps[0])

                def of_expert(t, e):
                    return t[:, e, :] if isinstance(e, int) else t[:, bass.ds(e, 1), :].rearrange("p a c -> p (a c)")

                def slots_out(e, par):
                    dve.wait_ge(s_xTp, e + 1)
                    v.tensor_copy(of_expert(goals, e), xe[:, par, :, C:ROW].rearrange("p j a -> p (j a)")).then_inc(s_goals, 1)
                    v.tensor_copy(xeT_hi[:, par, 0:512], bank_x[:, 0, :])
                    v.tensor_copy(xeT_hi[:, par, 512:CAP], bank_x[:, 1, 0:CAP - 512]).then_inc(s_xhi, 1)
                    dve.wait_ge(s_xhi, e + 1)
                    v.tensor_tensor(out=xeT_lo[:, par, 0:512], in0=bank_x[:, 0, :], in1=xeT_hi[:, par, 0:512], op=ALU.subtract)
                    v.tensor_tensor(out=xeT_lo[:, par, 512:CAP], in0=bank_x[:, 1, 0:CAP - 512],
                                    in1=xeT_hi[:, par, 512:CAP], op=ALU.subtract).then_inc(s_xT, 1)

                def split_w1(e, par):
                    dve.wait_ge(s_w1[par], e * 8 + (16 - 8 * par))
                    v.tensor_copy(w1_hi[:, par, :], w1[:, par, :]).then_inc(s_w1hi, 1)
                    dve.wait_ge(s_w1hi, e + 1)
                    v.tensor_tensor(out=w1_lo[:, par, :], in0=w1[:, par, :], in1=w1_hi[:, par, :],
                                    op=ALU.subtract).then_inc(s_w1s, 1)

                dve.wait_ge(s_routed, B)
                v.tensor_tensor(out=gap[:, :], in0=routed[:, 1, :], in1=routed[:, 0, :], op=ALU.subtract).then_inc(s_gap, 1)
                split_w1(0, 0)
                slots_out(0, 0)
                split_w1(1, 1)
                slots_out(1, 1)
                dve.wait_ge(s_b, 32)
                for k in range(TOPK):
                    last = v.tensor_scalar(kept[k][:, :], routed[:, 4 + k, :], float(CAP), None, ALU.is_lt)
                then(last)

                dve.wait_ge(s_egap, 1)
                then(v.tensor_scalar(denom[:, :], egap[:, :], 1.0, None, ALU.add))
                then(v.reciprocal(gate[0][:, :], denom[:, :]))
                then(v.tensor_tensor(out=gate[1][:, :], in0=gate[0][:, :], in1=egap[:, :], op=ALU.mult))
                for k in range(TOPK):
                    then(v.tensor_tensor(out=tmp[k][:, :], in0=gate[k][:, :], in1=kept[k][:, :], op=ALU.mult))
                then(v.tensor_tensor(out=denom[:, :], in0=tmp[0][:, :], in1=tmp[1][:, :], op=ALU.add))
                then(v.tensor_scalar(denom[:, :], denom[:, :], 1e-9, None, ALU.add))
                then(v.reciprocal(gap[:, :], denom[:, :]))
                for k in range(TOPK):
                    then(v.tensor_tensor(out=gate[k][:, :], in0=tmp[k][:, :], in1=gap[:, :], op=ALU.mult))
                dve.sem_inc(s_gates, 1)

                def add_bias(e, par):
                    bias = b2[:, e, :] if isinstance(e, int) else b2[:, bass.ds(e, 1), :].rearrange("p a c -> p (a c)")
                    if not isinstance(e, int) or e > 1:
                        wait(dve, s_store[par], e * (8 * SJ) - 8 * SJ * par)
                    dve.wait_ge(s_goals, e + 1)
                    v.tensor_copy(goal[:, par, :], of_expert(goals, e))
                    for part, (lo, n) in enumerate(((0, 4), (4, 1))):
                        dve.wait_ge(s_yp, e * 2 + (part + 1))
                        v.tensor_tensor(out=ye[:, par, lo:lo + n, :],
                                        in0=bank_y[:, part, 0:n * C].rearrange("p (j c) -> p j c", c=C),
                                        in1=bias[:, None, :].to_broadcast([P, n, C]), op=ALU.add).then_inc(s_ye, 1)

                for e in (2, 3):
                    split_w1(e, e % 2)
                    slots_out(e, e % 2)
                    add_bias(e - 2, e % 2)
                with dve.Fori(1, E // 2 - 1) as k:
                    for e, par in ((k * 2 + 2, 0), (k * 2 + 3, 1)):
                        split_w1(e, par)
                        slots_out(e, par)
                        add_bias(e - 2, par)
                add_bias(E - 2, 0)
                add_bias(E - 1, 1)

                with dve.Fori(0, B // 2) as k:
                    for par in range(2):
                        b = k * 2 + par
                        dve.wait_ge(s_rows[par], k * (16 * TOPK) + 16 * TOPK)
                        settle(dve, s_mark)
                        for i in range(TPB):
                            row = tile(rows[0], b, i)
                            last = v.scalar_tensor_tensor(out=row, in0=row, scalar=tile(gate[0], b, i), in1=tile(x, b, i),
                                                          op0=ALU.mult, op1=ALU.add)
                        last.then_inc(s_mid, 1)
                        dve.wait_ge(s_mid, b + 1)
                        dve.wait_ge(s_second, b + 1)
                        v.tensor_tensor(out=tiles_of(rows[0], b), in0=tiles_of(rows[0], b), in1=tiles_of(rows[1], b),
                                        op=ALU.add).then_inc(s_res, 1)

            @block.scalar
            def _(act):
                a = nc.scalar
                act.wait_ge(s_gap, 1)
                a.activation(egap[:, :], gap[:, :], ACT.Exp).then_inc(s_egap, 1)
                act.wait_ge(s_b, 32)
                with act.Fori(0, E // 2) as k:
                    for par in range(2):
                        e = k * 2 + par
                        for c in range(FC):
                            act.wait_ge(s_hp, e * 4 + (c + 1))
                            settle(act, s_mark)
                            a.activation(hT[:, par, c, :].rearrange("p (h k) -> p h k", h=2), bank_h[:, c % 2, :, 0:HALF],
                                         ACT.Gelu, bias=b1[:, bass.ds(e * FC + c, 1)]).then_inc(s_h, 1)
                act.wait_ge(s_gates, 1)
                with act.Fori(0, B // 2) as k:
                    for par in range(2):
                        b = k * 2 + par
                        act.wait_ge(s_rows[par], k * (16 * TOPK) + 16 * TOPK)
                        settle(act, s_mark)
                        for i in range(TPB):
                            row = tile(rows[1], b, i)
                            last = a.activation(row, row, ACT.Copy, scale=tile(gate[1], b, i))
                        last.then_inc(s_second, 1)

            @block.tensor
            def _(pe):
                t = nc.tensor
                def slots_in(e, par):
                    pe.wait_ge(s_xe[par], e * 8 + (16 - 8 * par))
                    wait(pe, s_xT, e)
                    for j in range(SJ):
                        last = t.transpose(bank_x[:, j // 4, (j % 4) * P:(j % 4 + 1) * P], xe[:, par, j, 0:C], ident[:, :])
                    last.then_inc(s_xTp, 1)

                def hidden(e, par, chunks):
                    if 0 in chunks:
                        pe.wait_ge(s_xT, e + 1)
                        pe.wait_ge(s_w1s, e + 1)
                    for c in chunks:
                        wait(pe, s_h, e * 4 + (c - 1))
                        chunk = slice(c * P, (c + 1) * P)
                        for hf in range(2):
                            cols = slice(hf * HALF, (hf + 1) * HALF)
                            for a, b in ((w1_hi, xeT_hi), (w1_hi, xeT_lo), (w1_lo, xeT_hi)):
                                last = t.matmul(bank_h[:, c % 2, hf, 0:HALF], a[:, par, chunk], b[:, par, cols],
                                                start=(b is xeT_hi and a is w1_hi), stop=(a is w1_lo))
                        last.then_inc(s_hp, 1)

                def outputs(e, par, tiles):
                    if 0 in tiles:
                        pe.wait_ge(s_h, e * 4 + 4)
                        pe.wait_ge(s_w2[par], e * 8 + (16 - 8 * par))
                        pe.wait_ge(s_ye, e * 2 + 1)
                    for j in tiles:
                        for c in range(FC):
                            last = t.matmul(bank_y[:, j // 4, (j % 4) * C:(j % 4 + 1) * C], hT[:, par, c, j * P:(j + 1) * P],
                                            w2[:, par, c, :], start=(c == 0), stop=(c == FC - 1))
                        if j >= 3:
                            last.then_inc(s_yp, 1)

                slots_in(0, 0)
                hidden(0, 0, range(FC))
                slots_in(1, 1)
                with pe.Fori(0, E // 2 - 1) as k:
                    for e, par in ((k * 2 + 1, 1), (k * 2 + 2, 0)):
                        hidden(e, par, (0, 1))
                        outputs(e - 1, 1 - par, (0, 1))
                        hidden(e, par, (2,))
                        outputs(e - 1, 1 - par, (2,))
                        hidden(e, par, (3,))
                        slots_in(e + 1, 1 - par)
                        outputs(e - 1, 1 - par, (3, 4))
                hidden(E - 1, 1, (0, 1))
                outputs(E - 2, 0, (0, 1))
                hidden(E - 1, 1, (2, 3))
                outputs(E - 2, 0, range(2, SJ))
                outputs(E - 1, 1, range(SJ))


def rope_tables():
    import numpy as np
    inv_freq = np.float32(1.0) / np.float32(10000.0) ** (np.arange(0, D, 2, dtype=np.float32) / np.float32(D))
    angle = np.arange(T, dtype=np.float32)[:, None] * inv_freq
    cos, sin = np.cos(angle), np.sin(angle)

    def tiles(a):
        return np.ascontiguousarray(a.reshape(TPB, P, D).transpose(1, 0, 2)).astype(np.float32)

    return tiles(np.concatenate([cos, cos], axis=1)), tiles(np.concatenate([-sin, sin], axis=1))


def kernel(L0_attn_x, L0_attn_wqkv, L0_attn_wo, L0_attn_q_norm_w, L0_attn_k_norm_w, L0_ffn_router_w,
           L0_ffn_router_b, L0_ffn_w1, L0_ffn_b1, L0_ffn_w2, L0_ffn_b2):
    import numpy as np
    import concourse.bacc as bacc
    from concourse.bass_utils import run_bass_kernel_spmd

    cos, sin = rope_tables()
    laid = {
        "x": np.ascontiguousarray(L0_attn_x),
        "wqkv": np.ascontiguousarray(np.asarray(L0_attn_wqkv).reshape(3, NP, P, C).transpose(3, 1, 0, 2).reshape(C, NP, QKV)),
        "wo": np.ascontiguousarray(np.asarray(L0_attn_wo).reshape(C, NP, P).transpose(2, 1, 0)),
        "q_norm_w": np.ascontiguousarray(L0_attn_q_norm_w),
        "k_norm_w": np.ascontiguousarray(L0_attn_k_norm_w),
        "router_w": np.ascontiguousarray(np.asarray(L0_ffn_router_w).T),
        "router_b": np.ascontiguousarray(L0_ffn_router_b),
        "w1": np.ascontiguousarray(L0_ffn_w1),
        "b1": np.ascontiguousarray(np.asarray(L0_ffn_b1).reshape(E * FC, P).T),
        "w2": np.ascontiguousarray(L0_ffn_w2),
        "b2": np.ascontiguousarray(L0_ffn_b2),
        "cos": cos,
        "sin": sin,
    }
    nc = bacc.Bacc("TRN2", target_bir_lowering=False, num_devices=1)
    args = [nc.dram_tensor(f"in_{n}", a.shape, mybir.dt.from_np(a.dtype), kind="ExternalInput").ap() for n, a in laid.items()]
    out = nc.dram_tensor("out_0", (B, T, C), F32, kind="ExternalOutput").ap()
    build(nc, *args, out)
    r = run_bass_kernel_spmd(nc, [{f"in_{n}": a for n, a in laid.items()}], core_ids=[0])
    return r.results[0]["out_0"]
```
